# Optimizing a Trainium2 kernel written in Bass

```python
import numpy as np
import jax
import jax.numpy as jnp

def _softmax(x, axis=-1):
    return jax.nn.softmax(x, axis=axis)

def _gelu(x):
    return jax.nn.gelu(x, approximate=True)

def _silu(x):
    return jax.nn.silu(x)

def _sigmoid(x):
    return jax.nn.sigmoid(x)

def _layernorm(x, axis=-1, eps=1e-05):
    m = jnp.mean(x, axis=axis, keepdims=True)
    v = jnp.var(x, axis=axis, keepdims=True)
    return (x - m) / jnp.sqrt(v + eps)

def _scatter_add(tgt, idx, src, axis=0):
    return tgt.at[idx].add(src)

def _segment_sum(src, seg, n):
    return jax.ops.segment_sum(src, seg, n)
kernel_name = 'mk_cond_seq_d1_seqx_r8_fb9be7'

def setup_inputs(seed: int=0):
    np.random.seed(seed)
    _w = jnp.asarray

    def _rec_inputs():
        import jax
        import jax.numpy as jnp
        _rk = jax.random.key(seed)
        x = -0.0003482 + 1 * jax.random.normal(jax.random.fold_in(_rk, 1), (32, 128, 144), jnp.float32)
        _lenS = 128 - jax.random.randint(jax.random.fold_in(_rk, 7), (32,), 0, max(1, 128 // 4) + 1, jnp.int32)
        _lenS2 = 128 - jax.random.randint(jax.random.fold_in(_rk, 8), (32,), 0, max(1, 128 // 4) + 1, jnp.int32)
        cond_1152 = -0.00342701 + 1.00097 * jax.random.normal(jax.random.fold_in(_rk, 11), (32, 144), jnp.float32)
        return (x, cond_1152)
    x, cond_1152 = _rec_inputs()

    def _L0_cond_setup():
        import jax, jax.numpy as jnp
        import numpy as np
        B, T, D, H = (64, 32, 144, 16)
        HD = D // H
        EPS = 1e-06

        def _ln(x):
            mu = jnp.mean(x, axis=-1, keepdims=True)
            var = jnp.var(x, axis=-1, keepdims=True)
            return (x - mu) * jax.lax.rsqrt(var + EPS)

        def _modulate(x, shift, scale):
            return x * (1.0 + scale[:, None, :]) + shift[:, None, :]

        def _attn(x, Wq, Wk, Wv, Wp, bp):
            b, t, d = x.shape
            q = (x @ Wq).reshape(b, t, H, HD).transpose(0, 2, 1, 3)
            k = (x @ Wk).reshape(b, t, H, HD).transpose(0, 2, 1, 3)
            v = (x @ Wv).reshape(b, t, H, HD).transpose(0, 2, 1, 3)
            scores = jnp.einsum('bhqd,bhkd->bhqk', q, k) / np.sqrt(HD)
            mask = jnp.triu(jnp.ones((t, t), bool), k=1)
            scores = jnp.where(mask, -jnp.inf, scores)
            w = jax.nn.softmax(scores, axis=-1)
            ctx = jnp.einsum('bhqk,bhkd->bhqd', w, v).transpose(0, 2, 1, 3).reshape(b, t, d)
            return ctx @ Wp + bp

        def _mlp(x, W1, b1, W2, b2):
            return jax.nn.silu(x @ W1 + b1) @ W2 + b2
        key = jax.random.key(seed)
        ks = jax.random.split(key, 12)
        s = lambda fan_in: 1.0 / np.sqrt(fan_in)
        return {'x': jax.random.normal(ks[0], (B, T, D), jnp.float32), 'c': jax.random.normal(ks[1], (B, D), jnp.float32), 'Wq': jax.random.normal(ks[2], (D, D), jnp.float32) * s(D), 'Wk': jax.random.normal(ks[3], (D, D), jnp.float32) * s(D), 'Wv': jax.random.normal(ks[4], (D, D), jnp.float32) * s(D), 'Wp': jax.random.normal(ks[5], (D, D), jnp.float32) * s(D), 'bp': jnp.zeros((D,), jnp.float32), 'W1': jax.random.normal(ks[6], (D, 4 * D), jnp.float32) * s(D), 'b1': jnp.zeros((4 * D,), jnp.float32), 'W2': jax.random.normal(ks[7], (4 * D, D), jnp.float32) * s(4 * D), 'b2': jnp.zeros((D,), jnp.float32), 'Wa': jax.random.normal(ks[8], (D, 6 * D), jnp.float32) * s(D), 'ba': jnp.zeros((6 * D,), jnp.float32)}
    _L0_cond_all = _L0_cond_setup()
    _L0_cond_in = {k: v for k, v in _L0_cond_all.items() if k in ('Wq', 'Wk', 'Wv', 'Wp', 'bp', 'W1', 'b1', 'W2', 'b2', 'Wa', 'ba')}
    del _L0_cond_all
    return {'x': x, 'cond_1152': cond_1152, 'L0_cond_Wq': _L0_cond_in['Wq'], 'L0_cond_Wk': _L0_cond_in['Wk'], 'L0_cond_Wv': _L0_cond_in['Wv'], 'L0_cond_Wp': _L0_cond_in['Wp'], 'L0_cond_bp': _L0_cond_in['bp'], 'L0_cond_W1': _L0_cond_in['W1'], 'L0_cond_b1': _L0_cond_in['b1'], 'L0_cond_W2': _L0_cond_in['W2'], 'L0_cond_b2': _L0_cond_in['b2'], 'L0_cond_Wa': _L0_cond_in['Wa'], 'L0_cond_ba': _L0_cond_in['ba']}

def reference(x, cond_1152, L0_cond_Wq, L0_cond_Wk, L0_cond_Wv, L0_cond_Wp, L0_cond_bp, L0_cond_W1, L0_cond_b1, L0_cond_W2, L0_cond_b2, L0_cond_Wa, L0_cond_ba):
    import jax
    import jax.numpy as jnp

    def _L0_cond_ref(x, c, Wq, Wk, Wv, Wp, bp, W1, b1, W2, b2, Wa, ba):
        import jax, jax.numpy as jnp
        import numpy as np
        B, T, D, H = (64, 32, 144, 16)
        HD = D // H
        EPS = 1e-06

        def _ln(x):
            mu = jnp.mean(x, axis=-1, keepdims=True)
            var = jnp.var(x, axis=-1, keepdims=True)
            return (x - mu) * jax.lax.rsqrt(var + EPS)

        def _modulate(x, shift, scale):
            return x * (1.0 + scale[:, None, :]) + shift[:, None, :]

        def _attn(x, Wq, Wk, Wv, Wp, bp):
            b, t, d = x.shape
            q = (x @ Wq).reshape(b, t, H, HD).transpose(0, 2, 1, 3)
            k = (x @ Wk).reshape(b, t, H, HD).transpose(0, 2, 1, 3)
            v = (x @ Wv).reshape(b, t, H, HD).transpose(0, 2, 1, 3)
            scores = jnp.einsum('bhqd,bhkd->bhqk', q, k) / np.sqrt(HD)
            mask = jnp.triu(jnp.ones((t, t), bool), k=1)
            scores = jnp.where(mask, -jnp.inf, scores)
            w = jax.nn.softmax(scores, axis=-1)
            ctx = jnp.einsum('bhqk,bhkd->bhqd', w, v).transpose(0, 2, 1, 3).reshape(b, t, d)
            return ctx @ Wp + bp

        def _mlp(x, W1, b1, W2, b2):
            return jax.nn.silu(x @ W1 + b1) @ W2 + b2
        mod = jax.nn.silu(c) @ Wa + ba
        sh_msa, sc_msa, g_msa, sh_mlp, sc_mlp, g_mlp = jnp.split(mod, 6, axis=1)
        x = x + g_msa[:, None, :] * _attn(_modulate(_ln(x), sh_msa, sc_msa), Wq, Wk, Wv, Wp, bp)
        x = x + g_mlp[:, None, :] * _mlp(_modulate(_ln(x), sh_mlp, sc_mlp), W1, b1, W2, b2)
        return x
    x = _L0_cond_ref(x, cond_1152, L0_cond_Wq, L0_cond_Wk, L0_cond_Wv, L0_cond_Wp, L0_cond_bp, L0_cond_W1, L0_cond_b1, L0_cond_W2, L0_cond_b2, L0_cond_Wa, L0_cond_ba)
    return x

_drawn_inputs = setup_inputs


def setup_inputs(seed=0):
    import zlib

    import numpy as np

    out = dict(_drawn_inputs(seed))
    spreads = {'L0_cond_bp': (0.0, 0.1),
     'L0_cond_b1': (0.0, 0.1),
     'L0_cond_b2': (0.0, 0.1),
     'L0_cond_ba': (0.0, 0.1)}
    factors = {}
    for name, (base, spread) in spreads.items():
        noise = np.random.default_rng([zlib.crc32(name.encode()), seed]).standard_normal(out[name].shape)
        drawn = base * np.exp(spread * noise) if base else spread * noise
        out[name] = jnp.asarray(drawn.astype(out[name].dtype))
    for name, factor in factors.items():
        out[name] = (out[name] * factor).astype(out[name].dtype)
    return out
```

```python
from contextlib import ExitStack

import numpy as np

import concourse.bass as bass
from concourse import mybir

F32 = mybir.dt.float32
F32R = mybir.dt.float32r
BF16 = mybir.dt.bfloat16
ALU = mybir.AluOpType
ACT = mybir.ActivationFunctionType
AX = mybir.AxisListType

NB, T, D = 32, 128, 144
H = 16
HD = D // H
FF = 4 * D
EPS = 1e-6
SCALE = float(1.0 / np.sqrt(HD))
KA = 128
KB = D - KA
HH = H // 2
FC = (FF + 127) // 128
FL = FF - (FC - 1) * 128
MASKED = -3.0e38
Y_LO_B, Y_HI_B, Y_LO_A = D, D + KB, D + 2 * KB
YW = D + 2 * KB + KA
HS = 64


def slots(q, k):
    return q * HD, H * HS + (k - q) * HD


def build(nc, x, cond, Wq, Wk, Wv, Wp, bp, W1, b1, W2, b2, Wa, ba, out):
    mod_dram = nc.dram_tensor("modulation", [NB, 6 * D], F32, kind="Internal").ap()
    ctx = ExitStack()
    with ctx:
        def sb(name, shape, dt=F32):
            return ctx.enter_context(nc.sbuf_tensor(name, shape, dt))

        def sem(name):
            return ctx.enter_context(nc.semaphore(name))

        def view(t, offset, dims, parts=128):
            width = int(np.prod(t.shape[1:]))
            return bass.AP(t, offset, [[width, parts], *dims])

        def slot_pair(p, q, k):
            offset, step = slots(q, k)
            return view(stack[p], offset, [[step, 2], [HS, H], [1, HD]])

        identf = sb("identf", [128, 128])
        identb = sb("identb", [128, 128], BF16)
        mask = sb("mask", [128, 128], BF16)
        pick = sb("pick", [128, HH, 128], BF16)
        wqkv = sb("wqkv", [128, 3 * D])
        wqkv_tail = sb("wqkv_tail", [3 * KB, 3 * D])
        w1 = sb("w1", [128, FF])
        w1_tail = sb("w1_tail", [3 * KB, FF])
        wqkv_hi = sb("wqkv_hi", [128, 3 * D], F32R)
        wqkv_lo = sb("wqkv_lo", [128, 3 * D], F32R)
        wqkv_rest = sb("wqkv_rest", [3 * KB, 3 * D], F32R)
        w1_hi = sb("w1_hi", [128, FF], F32R)
        w1_lo = sb("w1_lo", [128, FF], F32R)
        w1_rest = sb("w1_rest", [3 * KB, FF], F32R)
        wp_a = sb("wp_a", [128, D])
        wp_b = sb("wp_b", [KB + 1, D])
        w2 = sb("w2", [128, FC, D])
        b1c = sb("b1c", [128, FC])
        wa_a = sb("wa_a", [128, 6 * D])
        wa_b = sb("wa_b", [KB + 1, 6 * D])
        cond_sb = sb("cond_sb", [NB, D])
        cond_silu = sb("cond_silu", [NB, D + 1])
        condT = sb("condT", [128, 2, NB])
        mod = sb("mod", [NB, 6 * D])
        xr = sb("xr", [128, NB, D])
        st1 = sb("st1", [128, NB, 6])
        st2 = sb("st2", [128, NB, 6])
        mv = sb("mv", [128, NB, 2])
        ve = sb("ve", [128, NB])
        sd = sb("sd", [128, NB])
        rsd = sb("rsd", [128, NB])
        rstd = sb("rstd", [128, NB])
        nmr = sb("nmr", [128, NB])
        bcm = [sb(f"bcm{p}", [128, 2 * D]) for p in range(2)]
        bcg = [sb(f"bcg{p}", [128, D]) for p in range(2)]
        tn = [sb(f"tn{p}", [128, D]) for p in range(2)]
        ts = [sb(f"ts{p}", [128, D]) for p in range(2)]
        ym = [sb(f"ym{p}", [128, D]) for p in range(2)]
        y3 = [sb(f"y3{p}", [128, YW], F32R) for p in range(2)]
        yT = [sb(f"yT{p}", [128, 3, 256], F32R) for p in range(2)]
        stack = [sb(f"stack{p}", [128, 2 * H * HS], BF16) for p in range(2)]
        resid = [sb(f"resid{p}", [128, 2 * D]) for p in range(2)]
        vx = [sb(f"vx{p}", [128, H, HD + 1]) for p in range(2)]
        qkT = [sb(f"qkT{p}", [128, 2, HH, 128], BF16) for p in range(2)]
        mx = sb("mx", [128, 2, HH])
        mm = [sb(f"mm{h}", [128, 128], BF16) for h in range(2)]
        mT = [sb(f"mT{h}", [128, 128], BF16) for h in range(2)]
        P = [sb(f"P{h}", [128, HH, 128]) for h in range(2)]
        ctxT = sb("ctxT", [128, 4, 128])
        rden = sb("rden", [128, H])
        ctxn = sb("ctxn", [128, D + 1])
        backT = sb("backT", [128, 2, 128])
        gated = sb("gated", [128, D])
        hT = [sb(f"hT{p}", [128, FC, 256]) for p in range(2)]
        gated2 = [sb(f"gated2{t}", [128, D]) for t in range(2)]

        bank = [ctx.enter_context(nc.psum_tensor(f"bank{i}", [128, 512], F32)) for i in range(8)]
        B_XT, B_QKV, B_QKT, B_CTX = 0, 1, 2, 7
        S_BANK = (3, 4)
        ST_BANK = (5, 6)
        H_BANK = (2, 3, 4, 7, 2)

        s = {n: sem(n) for n in (
            "x_in0 x_in1 x_in2 x_in3 cond_in wa_in wqkv_in w1_in wp_in w2_in b1_in "
            "mod_out bcm_in0 bcm_in1 bcg_in0 bcg_in1 out_done "
            "consts vconsts cond_act cond_T condT_ev mod_mm mod_ev weights "
            "stats aggr ve_ready sd_ready nchain norm_ready "
            "t_ready scaled ym_ready yhi_ready y_ready xT_done yT_ready qkv_done v_ready qkv_read resid_ready "
            "mid_ready stack_ready dup_ready qT_done kT_done qTev kTev "
            "s_done max_done mhi mm_ready mT_done mT_ev st_done exp_done p_ready pv_done "
            "ctxT_ev tok_done rden_ready ctxn_ready back_done back_ev wp_done gated_ready gated_read x1_ready stats2 "
            "bc2_in0 bc2_in1 t2_ready scaled2 ym2_ready yhi2_ready y2_ready xT2_done yT2_ready w1_done silu_done w2_done "
            "gated2_ready result_ready").split()}

        def due(count):
            return not (isinstance(count, int) and count <= 0)

        def later(i, p, d):
            return i + (p + d) // 2, (p + d) % 2

        def sequences(eng, step):
            step(0, 0, False, True, True)
            step(0, 1, True, True, True)
            step(1, 0, True, True, True)
            with eng.Fori(1, (NB - 4) // 2) as i:
                step(i, 1, True, True, True)
                step(i + 1, 0, True, True, True)
            for b in range(NB - 3, NB):
                step(b // 2, b % 2, True, b + 1 < NB, b + 2 < NB)

        XG = NB // 4
        NPAIR = NB // 2
        block = ctx.enter_context(nc.Block())

        @block.sync
        def _(sp):
            sp.dma_start(cond_sb[:, :], cond).then_inc(s["cond_in"], 16)
            xv = x.rearrange("b t d -> t b d")
            sp.dma_start(xr[:, 0:XG, :], xv[:, 0:XG, :]).then_inc(s["x_in0"], 16)
            sp.dma_start(wa_a[:, :], Wa[0:KA, :]).then_inc(s["wa_in"], 16)
            sp.dma_start(wa_b[0:KB, :], Wa[KA:D, :]).then_inc(s["wa_in"], 16)
            sp.dma_start(wa_b[KB:KB + 1, :], ba.unsqueeze(0)).then_inc(s["wa_in"], 16)
            for g in range(1, 4):
                sp.dma_start(xr[:, g * XG:(g + 1) * XG, :], xv[:, g * XG:(g + 1) * XG, :])\
                    .then_inc(s[f"x_in{g}"], 16)
            for n, w in enumerate((Wq, Wk, Wv)):
                sp.dma_start(wqkv[:, n * D:(n + 1) * D], w[0:KA, :]).then_inc(s["wqkv_in"], 16)
                for r in range(3):
                    sp.dma_start(wqkv_tail[r * KB:(r + 1) * KB, n * D:(n + 1) * D], w[KA:D, :])\
                        .then_inc(s["wqkv_in"], 16)
            sp.dma_start(wp_a[:, :], Wp[0:KA, :]).then_inc(s["wp_in"], 16)
            sp.dma_start(wp_b[0:KB, :], Wp[KA:D, :]).then_inc(s["wp_in"], 16)
            sp.dma_start(wp_b[KB:KB + 1, :], bp.unsqueeze(0)).then_inc(s["wp_in"], 16)
            sp.dma_start(w1[:, :], W1[0:KA, :]).then_inc(s["w1_in"], 16)
            for r in range(3):
                sp.dma_start(w1_tail[r * KB:(r + 1) * KB, :], W1[KA:D, :]).then_inc(s["w1_in"], 16)
            sp.dma_start(w2[:, 0:FC - 1, :], W2[0:(FC - 1) * 128, :].rearrange("(c p) d -> p c d", p=128))\
                .then_inc(s["w2_in"], 16)
            sp.dma_start(w2[0:FL, FC - 1, :], W2[(FC - 1) * 128:FF, :]).then_inc(s["w2_in"], 16)
            sp.dma_start(w2[FL:FL + 1, FC - 1, :], b2.unsqueeze(0)).then_inc(s["w2_in"], 16)
            with nc.allow_non_contiguous_dma(reason="the bias of the hidden layer, one element a partition"):
                sp.dma_start(b1c[:, 0:FC - 1], b1[0:(FC - 1) * 128].rearrange("(c p) -> p c", p=128))\
                    .then_inc(s["b1_in"], 16)
                sp.dma_start(b1c[0:FL, FC - 1:FC], b1[(FC - 1) * 128:FF].unsqueeze(1)).then_inc(s["b1_in"], 16)
            sp.wait_ge(s["mod_ev"], 3)
            sp.dma_start(mod_dram, mod[:, :]).then_inc(s["mod_out"], 16)
            sp.wait_ge(s["mod_out"], 16)

            def row(b, lo, n):
                return mod_dram[bass.ds(b, 1), lo:lo + n].to_broadcast([128, n]) if not isinstance(b, int) \
                    else mod_dram[b:b + 1, lo:lo + n].to_broadcast([128, n])

            def load_modulation(i, p):
                b = 2 * i + p
                if due(b - 1):
                    sp.wait_ge(s["ym_ready"], b - 1)
                sp.dma_start(bcm[p][:, :], row(b, 0, 2 * D)).then_inc(s[f"bcm_in{p}"], 16)

            def step(i, p, tail, front, ahead):
                b = 2 * i + p
                if ahead:
                    load_modulation(*later(i, p, 2))
                if due(b - 1):
                    sp.wait_ge(s["gated_read"], b - 1)
                sp.dma_start(bcg[p][:, :], row(b, 2 * D, D)).then_inc(s[f"bcg_in{p}"], 16)

            load_modulation(0, 0)
            load_modulation(0, 1)
            sequences(sp, step)

            def load2(j, t):
                b = 2 * j + t
                if due(b - 1):
                    sp.wait_ge(s["ym2_ready"], b - 1)
                sp.dma_start(bcm[t][:, :], row(b, 3 * D, 2 * D)).then_inc(s[f"bc2_in{t}"], 16)

            def gate2(j, t):
                b = 2 * j + t
                if due(b - 1):
                    sp.wait_ge(s["gated2_ready"], b - 1)
                sp.dma_start(bcg[t][:, :], row(b, 5 * D, D)).then_inc(s[f"bcg_in{t}"], 16)

            sp.wait_ge(s["ym_ready"], NB)
            sp.wait_ge(s["gated_read"], NB)
            load2(0, 0)
            load2(0, 1)

            def pair2(j, last):
                if not last:
                    load2(j + 1, 0)
                    load2(j + 1, 1)
                gate2(j, 0)
                gate2(j, 1)

            pair2(0, False)
            with sp.Fori(1, NPAIR - 1) as j:
                pair2(j, False)
                sp.wait_ge(s["result_ready"], 2 * j)
                sp.dma_start(out.rearrange("b t d -> t b d")[:, bass.ds(2 * j - 2, 2), :],
                             xr[:, bass.ds(2 * j - 2, 2), :]).then_inc(s["out_done"], 16)
            pair2(NPAIR - 1, True)
            for j in (NPAIR - 2, NPAIR - 1):
                sp.wait_ge(s["result_ready"], 2 * j + 2)
                sp.dma_start(out.rearrange("b t d -> t b d")[:, 2 * j:2 * j + 2, :],
                             xr[:, 2 * j:2 * j + 2, :]).then_inc(s["out_done"], 16)
            sp.wait_ge(s["out_done"], 16 * NPAIR)

        @block.gpsimd
        def _(pool):
            g = nc.gpsimd
            g.memset(identf[:, :], 0.0)
            g.memset(identb[:, :], 0.0)
            g.memset(mask[:, :], 0.0)
            g.memset(pick[:, :, :], 0.0)
            g.memset(vx[0][:, :, :], 1.0)
            g.memset(vx[1][:, :, :], 1.0)
            g.memset(mm[0][:, :], 0.0)
            g.memset(mm[1][:, :], 0.0)
            g.memset(stack[0][:, :], 0.0)
            g.memset(stack[1][:, :], 0.0)
            g.memset(ctxn[:, D:D + 1], 1.0).then_inc(s["consts"], 1)
            pool.wait_ge(s["consts"], 1)
            for m in (identf, identb):
                g.affine_select(out=m[:, :], in_=m[:, :], compare_op=ALU.not_equal, fill=1.0, base=0,
                                pattern=[[-1, 128]], channel_multiplier=1)
            g.affine_select(out=mask[:, :], in_=mask[:, :], compare_op=ALU.is_ge, fill=MASKED, base=0,
                            pattern=[[-1, 128]], channel_multiplier=1)
            g.affine_select(out=pick[:, :, :], in_=pick[:, :, :], compare_op=ALU.not_equal, fill=-1.0,
                            base=0, pattern=[[-1, HH], [0, 128]], channel_multiplier=1)\
                .then_inc(s["consts"], 1)
            pool.wait_ge(s["consts"], 2)
            g.affine_select(out=pick[:, :, :], in_=pick[:, :, :], compare_op=ALU.not_equal, fill=-1.0,
                            base=-HH, pattern=[[-1, HH], [0, 128]], channel_multiplier=1)\
                .then_inc(s["consts"], 1)

            def standing():
                pool.nop(nofuse=True)

            def modulate(b, p, ready, arrived, count, scaled, ym_ready, yhi, y_ready, used, used_count):
                pool.wait_ge(s[arrived], count)
                pool.wait_ge(s[ready], b + 1)
                g.tensor_tensor(ts[p][:, :], tn[p][:, :], bcm[p][:, D:2 * D], ALU.mult).then_inc(s[scaled], 1)
                pool.wait_ge(s[scaled], b + 1)
                g.tensor_tensor(ym[p][:, :], ts[p][:, :], bcm[p][:, 0:D], ALU.add).then_inc(s[ym_ready], 1)
                pool.wait_ge(s[ym_ready], b + 1)
                if due(used_count):
                    pool.wait_ge(s[used], used_count)
                standing()
                g.tensor_scalar(y3[p][:, 0:D], ym[p][:, :], 1.0, 0.0, ALU.mult, ALU.add).then_inc(s[yhi], 1)
                g.tensor_scalar(y3[p][:, Y_HI_B:Y_HI_B + KB], ym[p][:, KA:D], 1.0, 0.0, ALU.mult, ALU.add)
                pool.wait_ge(s[yhi], b + 1)
                g.tensor_tensor(y3[p][:, Y_LO_B:Y_LO_B + KB], ym[p][:, KA:D], y3[p][:, KA:D].bitcast(F32),
                                ALU.subtract)
                g.tensor_tensor(y3[p][:, Y_LO_A:YW], ym[p][:, 0:KA], y3[p][:, 0:KA].bitcast(F32), ALU.subtract)\
                    .then_inc(s[y_ready], 1)

            def modulate1(i, p):
                b = 2 * i + p
                modulate(b, p, "t_ready", f"bcm_in{p}", 16 * i + 16, "scaled", "ym_ready", "yhi_ready", "y_ready",
                         "xT_done", b - 1)

            def split(i, p):
                b = 2 * i + p
                pool.wait_ge(s["resid_ready"], b + 1)
                standing()
                r = view(resid[p], 0, [[D, 2], [HD, H], [1, HD]])
                mid = slot_pair(p, 2, 2)
                g.tensor_scalar(mid, r, 1.0, 0.0, ALU.mult, ALU.add).then_inc(s["mid_ready"], 1)
                g.tensor_scalar(slot_pair(p, 3, 1), r, 1.0, 0.0, ALU.mult, ALU.add)
                pool.wait_ge(s["mid_ready"], b + 1)
                g.tensor_tensor(slot_pair(p, 5, 4), r, mid, ALU.subtract).then_inc(s["stack_ready"], 1)

            def select(i, p, h):
                b = 2 * i + p
                pool.wait_ge(s["exp_done"], 2 * b + h + 1)
                standing()
                g.affine_select(out=P[h][:, :, :], in_=P[h][:, :, :], compare_op=ALU.is_ge, fill=0.0,
                                base=0, pattern=[[0, HH], [1, 128]], channel_multiplier=-1)\
                    .then_inc(s["p_ready"], 1)

            modulate1(0, 0)
            modulate1(0, 1)
            split(0, 0)

            def step(i, p, tail, front, ahead):
                if tail:
                    select(*later(i, p, -1), 1)
                if ahead:
                    modulate1(*later(i, p, 2))
                if front:
                    split(*later(i, p, 1))
                select(i, p, 0)

            sequences(pool, step)
            select(NPAIR - 1, 1, 1)

            def modulate2(j):
                for t in range(2):
                    b = 2 * j + t
                    modulate(b, t, "t2_ready", f"bc2_in{t}", 16 * j + 16, "scaled2", "ym2_ready", "yhi2_ready",
                             "y2_ready", "xT2_done", b - 1)

            modulate2(0)
            with pool.Fori(1, NPAIR) as j:
                modulate2(j)

        @block.scalar
        def _(act):
            a = nc.scalar
            act.wait_ge(s["vconsts"], 1)
            act.wait_ge(s["cond_in"], 16)
            a.activation(cond_silu[:, 0:D], cond_sb[:, :], ACT.Silu).then_inc(s["cond_act"], 1)
            act.wait_ge(s["cond_T"], 1)
            a.copy(condT[:, 0, :], bank[0][:, 0:NB])
            a.copy(condT[0:KB + 1, 1, :], bank[0][0:KB + 1, NB:2 * NB]).then_inc(s["condT_ev"], 1)
            act.wait_ge(s["ve_ready"], 1)
            a.activation(sd[:, :], ve[:, :], ACT.Sqrt).then_inc(s["sd_ready"], 1)

            def evacuate_y(i, p):
                b = 2 * i + p
                act.wait_ge(s["xT_done"], b + 1)
                a.copy(yT[p][:, 0:2, 0:128], bank[B_XT][:, 0:256].rearrange("p (c t) -> p c t", c=2))
                a.copy(yT[p][0:3 * KB, 2, 0:128], bank[B_XT][0:3 * KB, 256:384]).then_inc(s["yT_ready"], 1)

            def evacuate_qkv(i, p):
                b = 2 * i + p
                act.wait_ge(s["qkv_done"], b + 1)
                if due(b - 1):
                    act.wait_ge(s["kT_done"], b - 1)
                a.copy(slot_pair(p, 0, 0),
                       bank[B_QKV][:, 0:2 * D].rearrange("p (w h d) -> p w h d", w=2, h=H))
                if due(2 * b - 2):
                    act.wait_ge(s["pv_done"], 2 * b - 2)
                a.copy(vx[p][:, :, 0:HD], bank[B_QKV][:, 2 * D:3 * D].rearrange("p (h d) -> p h d", h=H))\
                    .then_inc(s["v_ready"], 1)

            def evacuate_mT(i, p, h):
                b = 2 * i + p
                act.wait_ge(s["mT_done"], 2 * b + h + 1)
                if due(2 * b + h - 1):
                    act.wait_ge(s["st_done"], 2 * b + h - 1)
                a.copy(mT[h][:, :], bank[B_XT][:, 384:448].bitcast(BF16)).then_inc(s["mT_ev"], 1)

            def exponentials(i, p, h):
                b = 2 * i + p
                act.wait_ge(s["st_done"], 2 * b + h + 1)
                if due(2 * b + h - 1):
                    act.wait_ge(s["pv_done"], 2 * b + h - 1)
                for n, k in enumerate(ST_BANK):
                    last = a.activation(P[h][:, n * HH // 2:(n + 1) * HH // 2, :],
                                        bank[k][:, :].rearrange("p (h t) -> p h t", t=128), ACT.Exp, scale=SCALE)
                last.then_inc(s["exp_done"], 1)

            def evacuate_ctx(i, p):
                b = 2 * i + p
                act.wait_ge(s["pv_done"], 2 * b + 2)
                if due(b):
                    act.wait_ge(s["tok_done"], b)
                a.copy(ctxT[:, :, :], bank[B_CTX][:, :].rearrange("p (g t) -> p g t", t=128))\
                    .then_inc(s["ctxT_ev"], 1)

            def evacuate_back(i, p):
                b = 2 * i + p
                act.wait_ge(s["back_done"], b + 1)
                if due(b):
                    act.wait_ge(s["wp_done"], b)
                a.copy(backT[:, 0, :], bank[B_CTX][:, 0:128])
                a.copy(backT[0:KB + 1, 1, :], bank[B_CTX][0:KB + 1, 128:256]).then_inc(s["back_ev"], 1)

            evacuate_y(0, 0)
            evacuate_qkv(0, 0)

            def step(i, p, tail, front, ahead):
                if front:
                    evacuate_y(*later(i, p, 1))
                if tail:
                    evacuate_ctx(*later(i, p, -1))
                if front:
                    evacuate_qkv(*later(i, p, 1))
                evacuate_mT(i, p, 0)
                exponentials(i, p, 0)
                evacuate_mT(i, p, 1)
                if tail:
                    evacuate_back(*later(i, p, -1))
                exponentials(i, p, 1)

            sequences(act, step)
            evacuate_ctx(NPAIR - 1, 1)
            evacuate_back(NPAIR - 1, 1)

            act.wait_ge(s["ve_ready"], 2)
            a.activation(sd[:, :], ve[:, :], ACT.Sqrt).then_inc(s["sd_ready"], 1)
            act.wait_ge(s["b1_in"], 32)

            def hidden(j, q):
                for c in range(FC):
                    n = 128 if c < FC - 1 else FL
                    act.wait_ge(s["w1_done"], FC * j + c + 1)
                    if c == 0:
                        if due(2 * j - 2):
                            act.wait_ge(s["w2_done"], 2 * j - 2)
                    a.activation(hT[q][0:n, c, :], bank[H_BANK[c]][0:n, 0:256], ACT.Silu,
                                 bias=b1c[0:n, c:c + 1]).then_inc(s["silu_done"], 1)

            hidden(0, 0)
            hidden(1, 1)
            with act.Fori(1, NPAIR // 2) as k:
                hidden(2 * k, 0)
                hidden(2 * k + 1, 1)

        @block.vector
        def _(dve):
            v = nc.vector
            v.memset(cond_silu[:, D:D + 1], 1.0)
            for q in range(2):
                v.memset(hT[q][FL:FL + 1, FC - 1, :], 1.0)
            v.memset(bank[B_CTX][:, :], 0.0).then_inc(s["vconsts"], 1)
            for n in range(4):
                dve.wait_ge(s[f"x_in{n}"], 16)
                with dve.Fori(n * XG, (n + 1) * XG) as b:
                    v.bn_stats(st1[:, bass.ds(b, 1), :], xr[:, bass.ds(b, 1), :]).then_inc(s["stats"], 1)

            def aggregate(st, nstats, done, times):
                dve.wait_ge(s[nstats], NB)
                for b in range(NB):
                    last = v.bn_aggr(mv[:, b, :], st[:, b, :])
                last.then_inc(s["aggr"], 1)
                dve.wait_ge(s["aggr"], times)
                v.tensor_scalar(ve[:, :], mv[:, :, 1], EPS, None, ALU.add).then_inc(s["ve_ready"], 1)

            def inverse_deviation(times):
                base = 4 * (times - 1)
                dve.wait_ge(s["sd_ready"], times)
                v.reciprocal(rsd[:, :], sd[:, :]).then_inc(s["nchain"], 1)
                dve.wait_ge(s["nchain"], base + 1)
                v.tensor_tensor(rsd[:, :], rsd[:, :], ve[:, :], ALU.mult).then_inc(s["nchain"], 1)
                dve.wait_ge(s["nchain"], base + 2)
                v.tensor_tensor(rsd[:, :], rsd[:, :], sd[:, :], ALU.add).then_inc(s["nchain"], 1)
                dve.wait_ge(s["nchain"], base + 3)
                v.reciprocal(rstd[:, :], rsd[:, :]).then_inc(s["nchain"], 1)
                dve.wait_ge(s["nchain"], base + 4)
                v.tensor_scalar(rstd[:, :], rstd[:, :], 2.0, None, ALU.mult).then_inc(s["norm_ready"], 1)
                dve.wait_ge(s["norm_ready"], 2 * times - 1)
                v.scalar_tensor_tensor(out=nmr[:, :], in0=mv[:, :, 0], scalar=-1.0, in1=rstd[:, :],
                                       op0=ALU.mult, op1=ALU.mult).then_inc(s["norm_ready"], 1)
                dve.wait_ge(s["norm_ready"], 2 * times)

            dve.wait_ge(s["mod_mm"], 1)
            for n in range(2):
                v.tensor_copy(mod[:, n * 3 * D:(n + 1) * 3 * D], bank[1 + n][0:NB, 0:3 * D]).then_inc(s["mod_ev"], 1)
            dve.wait_ge(s["mod_ev"], 2)
            v.tensor_scalar(mod[:, :].rearrange("p (n d) -> p n d", n=6)[:, 1:5:3, :],
                            mod[:, :].rearrange("p (n d) -> p n d", n=6)[:, 1:5:3, :], 1.0, None, ALU.add)\
                .then_inc(s["mod_ev"], 1)
            aggregate(st1, "stats", "aggr", 1)
            dve.wait_ge(s["wqkv_in"], 12 * 16)
            v.tensor_copy(wqkv_hi[:, :], wqkv[:, :])
            v.tensor_copy(wqkv_rest[:, :], wqkv_tail[:, :]).then_inc(s["weights"], 1)
            dve.wait_ge(s["weights"], 1)
            v.tensor_tensor(wqkv_lo[:, :], wqkv[:, :], wqkv_hi[:, :].bitcast(F32), ALU.subtract)
            v.tensor_tensor(wqkv_rest[2 * KB:3 * KB, :], wqkv_tail[2 * KB:3 * KB, :],
                            wqkv_rest[2 * KB:3 * KB, :].bitcast(F32), ALU.subtract).then_inc(s["weights"], 1)
            inverse_deviation(1)

            def normalize(b, p, name, used):
                if due(b - 1):
                    dve.wait_ge(s[used], b - 1)
                v.tensor_scalar(tn[p][:, :], xr[:, b, :] if isinstance(b, int) else xr[:, bass.ds(b, 1), :],
                                rstd[:, bass.ds(b, 1)], nmr[:, bass.ds(b, 1)], ALU.mult, ALU.add)\
                    .then_inc(s[name], 1)

            def residuals(i, p):
                b = 2 * i + p
                dve.wait_ge(s["v_ready"], b + 1)
                if due(b - 1):
                    dve.wait_ge(s["stack_ready"], b - 1)
                hi = slot_pair(p, 0, 0)
                v.tensor_tensor(resid[p][:, :].rearrange("p (w h d) -> p w h d", w=2, h=H),
                                bank[B_QKV][:, 0:2 * D].rearrange("p (w h d) -> p w h d", w=2, h=H),
                                hi, ALU.subtract).then_inc(s["resid_ready"], 1)
                v.tensor_copy(slot_pair(p, 1, 3), hi)
                v.tensor_copy(slot_pair(p, 4, 5), hi).then_inc(s["dup_ready"], 1)

            def maxima(i, p, h):
                b = 2 * i + p
                dve.wait_ge(s["s_done"], 2 * b + h + 1)
                for n, k in enumerate(S_BANK):
                    last = v.tensor_reduce(mx[:, h, n * HH // 2:(n + 1) * HH // 2],
                                           bank[k][:, :].rearrange("p (h t) -> p h t", t=128), AX.X, ALU.max)
                last.then_inc(s["max_done"], 1)
                dve.wait_ge(s["max_done"], 2 * b + h + 1)
                if due(2 * b + h - 1):
                    dve.wait_ge(s["mT_done"], 2 * b + h - 1)
                v.tensor_copy(mm[h][:, 0:HH], mx[:, h, :]).then_inc(s["mhi"], 1)
                dve.wait_ge(s["mhi"], 2 * b + h + 1)
                v.tensor_tensor(mm[h][:, HH:2 * HH], mx[:, h, :], mm[h][:, 0:HH], ALU.subtract)\
                    .then_inc(s["mm_ready"], 1)

            def evacuate_T(i, p, w):
                b = 2 * i + p
                dve.wait_ge(s[("qT_done", "kT_done")[w]], b + 1)
                if due(2 * b - 2):
                    dve.wait_ge(s["st_done"], 2 * b - 2)
                v.tensor_copy(qkT[p][:, w, :, :], bank[B_QKT][:, :].bitcast(BF16)
                              .rearrange("p (j t) -> p j t", t=128)).then_inc(s[("qTev", "kTev")[w]], 1)

            def divide(i, p):
                b = 2 * i + p
                tok = bank[B_CTX][:, :].rearrange("p (h c) -> p h c", c=32)
                dve.wait_ge(s["tok_done"], b + 1)
                v.reciprocal(rden[:, :], tok[:, :, HD]).then_inc(s["rden_ready"], 1)
                dve.wait_ge(s["rden_ready"], b + 1)
                if due(b):
                    dve.wait_ge(s["back_done"], b)
                v.tensor_tensor(ctxn[:, 0:D].rearrange("p (h d) -> p h d", d=HD), tok[:, :, 0:HD],
                                rden[:, :].unsqueeze(2).to_broadcast([128, H, HD]), ALU.mult)\
                    .then_inc(s["ctxn_ready"], 1)

            def add_attention(i, p):
                b = 2 * i + p
                dve.wait_ge(s["wp_done"], b + 1)
                dve.wait_ge(s[f"bcg_in{p}"], 16 * i + 16)
                v.tensor_tensor(gated[:, :], bank[B_CTX][:, 0:D], bcg[p][:, :], ALU.mult)\
                    .then_inc(s["gated_read"], 1)
                dve.wait_ge(s["gated_read"], b + 1)
                row = xr[:, bass.ds(b, 1), :]
                v.tensor_tensor(row, row, gated[:, :].unsqueeze(1), ALU.add).then_inc(s["x1_ready"], 1)
                dve.wait_ge(s["x1_ready"], b + 1)
                v.bn_stats(st2[:, bass.ds(b, 1), :], row).then_inc(s["stats2"], 1)

            normalize(0, 0, "t_ready", "scaled")
            normalize(1, 1, "t_ready", "scaled")
            residuals(0, 0)
            evacuate_T(0, 0, 0)
            evacuate_T(0, 0, 1)

            def step(i, p, tail, front, ahead):
                if ahead:
                    ia, pa = later(i, p, 2)
                    normalize(2 * ia + pa, pa, "t_ready", "scaled")
                maxima(i, p, 0)
                if front:
                    residuals(*later(i, p, 1))
                maxima(i, p, 1)
                if tail:
                    divide(*later(i, p, -1))
                if front:
                    evacuate_T(*later(i, p, 1), 0)
                if tail:
                    add_attention(*later(i, p, -1))
                if front:
                    evacuate_T(*later(i, p, 1), 1)

            sequences(dve, step)
            divide(NPAIR - 1, 1)
            add_attention(NPAIR - 1, 1)

            aggregate(st2, "stats2", "aggr", 2)
            dve.wait_ge(s["w1_in"], 4 * 16)
            v.tensor_copy(w1_hi[:, :], w1[:, :])
            v.tensor_copy(w1_rest[:, :], w1_tail[:, :]).then_inc(s["weights"], 1)
            dve.wait_ge(s["weights"], 3)
            v.tensor_tensor(w1_lo[:, :], w1[:, :], w1_hi[:, :].bitcast(F32), ALU.subtract)
            v.tensor_tensor(w1_rest[2 * KB:3 * KB, :], w1_tail[2 * KB:3 * KB, :],
                            w1_rest[2 * KB:3 * KB, :].bitcast(F32), ALU.subtract).then_inc(s["weights"], 1)
            inverse_deviation(2)
            dve.wait_ge(s["y_ready"], NB)

            def normalize2(j):
                for t in range(2):
                    normalize(2 * j + t, t, "t2_ready", "scaled2")

            def evacuate_y2(j, q):
                for t in range(2):
                    b = 2 * j + t
                    dve.wait_ge(s["xT2_done"], b + 1)
                    if t == 0:
                        if due(FC * j - FC):
                            dve.wait_ge(s["w1_done"], FC * j - FC)
                    v.tensor_copy(yT[q][:, 0:2, t * 128:(t + 1) * 128],
                                  bank[t][:, 0:256].rearrange("p (c t) -> p c t", c=2))
                    v.tensor_copy(yT[q][0:3 * KB, 2, t * 128:(t + 1) * 128], bank[t][0:3 * KB, 256:384])\
                        .then_inc(s["yT2_ready"], 1)

            def add_mlp(j):
                for t in range(2):
                    b = 2 * j + t
                    dve.wait_ge(s["w2_done"], b + 1)
                    dve.wait_ge(s[f"bcg_in{t}"], 16 * (NPAIR + 1) + 16 * j)
                    if due(b - 1):
                        dve.wait_ge(s["result_ready"], b - 1)
                    v.tensor_tensor(gated2[t][:, :], bank[5 + t][:, 0:D], bcg[t][:, :], ALU.mult)\
                        .then_inc(s["gated2_ready"], 1)
                for t in range(2):
                    b = 2 * j + t
                    dve.wait_ge(s["gated2_ready"], b + 1)
                    row = xr[:, bass.ds(b, 1), :]
                    v.tensor_tensor(row, row, gated2[t][:, :].unsqueeze(1), ALU.add).then_inc(s["result_ready"], 1)

            normalize2(0)
            evacuate_y2(0, 0)
            normalize2(1)

            def pair(j, q, front, ahead):
                if front:
                    evacuate_y2(j + 1, 1 - q)
                if ahead:
                    normalize2(j + 2)
                add_mlp(j)

            pair(0, 0, True, True)
            with dve.Fori(0, (NPAIR - 4) // 2) as k:
                pair(2 * k + 1, 1, True, True)
                pair(2 * k + 2, 0, True, True)
            pair(NPAIR - 3, 1, True, True)
            pair(NPAIR - 2, 0, True, False)
            pair(NPAIR - 1, 1, False, False)

        @block.tensor
        def _(pe):
            mmul = nc.tensor.matmul
            tr = nc.tensor.transpose
            pe.wait_ge(s["consts"], 3)
            pe.wait_ge(s["cond_act"], 1)
            tr(bank[0][:, 0:NB], cond_silu[:, 0:KA], identf[0:NB, 0:NB])
            tr(bank[0][0:KB + 1, NB:2 * NB], cond_silu[:, KA:D + 1], identf[0:NB, 0:NB]).then_inc(s["cond_T"], 1)
            pe.wait_ge(s["condT_ev"], 1)
            pe.wait_ge(s["wa_in"], 48)
            for n in range(2):
                cols = slice(n * 3 * D, (n + 1) * 3 * D)
                mmul(bank[1 + n][0:NB, 0:3 * D], condT[:, 0, :], wa_a[:, cols], start=True, stop=False)
                last = mmul(bank[1 + n][0:NB, 0:3 * D], condT[0:KB + 1, 1, :], wa_b[:, cols],
                            start=False, stop=True)
            last.then_inc(s["mod_mm"], 1)

            def transpose_y(dst, src):
                tr(dst[:, 0:128], src[:, 0:KA].bitcast(F32), identf[:, :])
                tr(dst[:, 128:256], src[:, Y_LO_A:YW].bitcast(F32), identf[:, :])
                return tr(dst[0:3 * KB, 256:384], src[:, KA:KA + 3 * KB].bitcast(F32), identf[:, :])

            def front_x(i, p):
                b = 2 * i + p
                pe.wait_ge(s["y_ready"], b + 1)
                if due(2 * b - 2):
                    pe.wait_ge(s["mT_ev"], 2 * b - 2)
                transpose_y(bank[B_XT], y3[p]).then_inc(s["xT_done"], 1)

            def front_qkv(i, p):
                b = 2 * i + p
                pe.wait_ge(s["yT_ready"], b + 1)
                if due(b):
                    pe.wait_ge(s["resid_ready"], b)
                if due(b):
                    pe.wait_ge(s["v_ready"], b)
                dst = bank[B_QKV][:, 0:3 * D]
                mmul(dst, yT[p][:, 0, 0:128], wqkv_hi[:, :], start=True, stop=False)
                mmul(dst, yT[p][:, 0, 0:128], wqkv_lo[:, :], start=False, stop=False)
                mmul(dst, yT[p][:, 1, 0:128], wqkv_hi[:, :], start=False, stop=False)
                mmul(dst, yT[p][0:3 * KB, 2, 0:128], wqkv_rest[:, :], start=False, stop=True)\
                    .then_inc(s["qkv_done"], 1)

            def front_T(i, p, w):
                b = 2 * i + p
                if w == 0:
                    pe.wait_ge(s["stack_ready"], b + 1)
                    pe.wait_ge(s["dup_ready"], b + 1)
                    if due(b):
                        pe.wait_ge(s["kTev"], b)
                else:
                    pe.wait_ge(s["qTev"], b + 1)
                dst = bank[B_QKT][:, :].bitcast(BF16)
                for j in range(HH):
                    src = stack[p][:, (w * H + 2 * j) * HS:(w * H + 2 * j + 2) * HS]
                    last = tr(dst[:, j * 128:(j + 1) * 128], src, identb[:, :])
                last.then_inc(s[("qT_done", "kT_done")[w]], 1)

            def operand(p, w, head):
                r = 64 * (head % 2)
                return qkT[p][r:r + 64, w, head // 2, :]

            def scores_by_query(i, p, h):
                b = 2 * i + p
                if h == 0:
                    pe.wait_ge(s["kTev"], b + 1)
                if due(2 * b + h):
                    pe.wait_ge(s["max_done"], 2 * b + h)
                for n, k in enumerate(S_BANK):
                    mmul(bank[k][:, :].rearrange("p (h t) -> p h t", t=128), identb[:, :],
                         mask[:, :].unsqueeze(1).to_broadcast([128, HH // 2, 128]),
                         start=True, stop=False, skip_group_check=True)
                for n, k in enumerate(S_BANK):
                    for c in range(HH // 2):
                        head = h * HH + 2 * c + n
                        last = mmul(bank[k][:, c * 128:(c + 1) * 128], operand(p, 0, head), operand(p, 1, head),
                                    start=False, stop=True, skip_group_check=True)
                last.then_inc(s["s_done"], 1)

            def transpose_m(i, p, h):
                b = 2 * i + p
                pe.wait_ge(s["mm_ready"], 2 * b + h + 1)
                if due(2 * b + h):
                    pe.wait_ge(s["mT_ev"], 2 * b + h)
                if h == 0:
                    pe.wait_ge(s["yT_ready"], b + 1)
                tr(bank[B_XT][:, 384:448].bitcast(BF16), mm[h][:, :], identb[:, :]).then_inc(s["mT_done"], 1)

            def scores_by_key(i, p, h):
                b = 2 * i + p
                pe.wait_ge(s["mT_ev"], 2 * b + h + 1)
                if due(2 * b + h):
                    pe.wait_ge(s["exp_done"], 2 * b + h)
                for n, k in enumerate(ST_BANK):
                    for c in range(HH // 2):
                        mmul(bank[k][:, c * 128:(c + 1) * 128], pick[:, n * HH // 2 + c, :], mT[h][:, :],
                             start=(c == 0), stop=False, skip_group_check=True)
                for n, k in enumerate(ST_BANK):
                    for c in range(HH // 2):
                        head = h * HH + 2 * c + n
                        last = mmul(bank[k][:, c * 128:(c + 1) * 128], operand(p, 1, head), operand(p, 0, head),
                                    start=False, stop=True, skip_group_check=True)
                last.then_inc(s["st_done"], 1)

            def weigh(i, p, h):
                b = 2 * i + p
                pe.wait_ge(s["p_ready"], 2 * b + h + 1)
                if h == 0:
                    if due(b):
                        pe.wait_ge(s["gated_read"], b)
                for g in range(2):
                    for q in range(4):
                        head = h * HH + 4 * g + q
                        slot = (head % 2) * (HH // 2) + (head % HH) // 2
                        last = mmul(bank[B_CTX][32 * q:32 * q + HD + 1, (2 * h + g) * 128:(2 * h + g + 1) * 128],
                                    vx[p][:, head, :], P[h][:, slot, :], start=True, stop=True)
                last.then_inc(s["pv_done"], 1)

            def context_by_token(i, p):
                b = 2 * i + p
                pe.wait_ge(s["ctxT_ev"], b + 1)
                for g in range(4):
                    last = tr(bank[B_CTX][:, g * 128:(g + 1) * 128], ctxT[:, g, :], identf[:, :])
                last.then_inc(s["tok_done"], 1)

            def context_back(i, p):
                b = 2 * i + p
                pe.wait_ge(s["ctxn_ready"], b + 1)
                tr(bank[B_CTX][:, 0:128], ctxn[:, 0:KA], identf[:, :])
                tr(bank[B_CTX][0:KB + 1, 128:256], ctxn[:, KA:D + 1], identf[:, :]).then_inc(s["back_done"], 1)

            def project(i, p):
                b = 2 * i + p
                pe.wait_ge(s["back_ev"], b + 1)
                mmul(bank[B_CTX][:, 0:D], backT[:, 0, :], wp_a[:, :], start=True, stop=False)
                mmul(bank[B_CTX][:, 0:D], backT[0:KB + 1, 1, :], wp_b[:, :], start=False, stop=True)\
                    .then_inc(s["wp_done"], 1)

            pe.wait_ge(s["mod_ev"], 2)
            front_x(0, 0)
            pe.wait_ge(s["weights"], 2)
            front_qkv(0, 0)
            front_T(0, 0, 0)
            front_T(0, 0, 1)
            pe.wait_ge(s["wp_in"], 48)

            def step(i, p, tail, front, ahead):
                scores_by_query(i, p, 0)
                if front:
                    front_x(*later(i, p, 1))
                if tail:
                    weigh(*later(i, p, -1), 1)
                if front:
                    front_qkv(*later(i, p, 1))
                scores_by_query(i, p, 1)
                if tail:
                    context_by_token(*later(i, p, -1))
                if front:
                    pe.wait_ge(s["yT_ready"], 2 * i + p + 2)
                transpose_m(i, p, 0)
                scores_by_key(i, p, 0)
                if tail:
                    context_back(*later(i, p, -1))
                transpose_m(i, p, 1)
                if front:
                    front_T(*later(i, p, 1), 0)
                scores_by_key(i, p, 1)
                if tail:
                    project(*later(i, p, -1))
                if front:
                    front_T(*later(i, p, 1), 1)
                weigh(i, p, 0)

            sequences(pe, step)
            last = (NPAIR - 1, 1)
            weigh(*last, 1)
            context_by_token(*last)
            context_back(*last)
            project(*last)

            pe.wait_ge(s["weights"], 4)
            pe.wait_ge(s["w2_in"], 48)

            def front_x2(j):
                for t in range(2):
                    b = 2 * j + t
                    pe.wait_ge(s["y2_ready"], b + 1)
                    if due(b - 1):
                        pe.wait_ge(s["yT2_ready"], b - 1)
                    transpose_y(bank[t], y3[t]).then_inc(s["xT2_done"], 1)

            def expand(j, q):
                pe.wait_ge(s["yT2_ready"], 2 * j + 2)
                for c in range(FC):
                    n = 128 if c < FC - 1 else FL
                    f = slice(c * 128, c * 128 + n)
                    dst = bank[H_BANK[c]][0:n, 0:256]
                    if due(FC * j + 1 if c == FC - 1 else FC * (j - 1) + (FC if c == 0 else c + 1)):
                        pe.wait_ge(s["silu_done"], FC * j + 1 if c == FC - 1 else FC * (j - 1) + (FC if c == 0 else c + 1))
                    mmul(dst, w1_hi[:, f], yT[q][:, 0, :], start=True, stop=False)
                    mmul(dst, w1_hi[:, f], yT[q][:, 1, :], start=False, stop=False)
                    mmul(dst, w1_lo[:, f], yT[q][:, 0, :], start=False, stop=False)
                    mmul(dst, w1_rest[:, f], yT[q][0:3 * KB, 2, :], start=False, stop=True)\
                        .then_inc(s["w1_done"], 1)

            def contract(j, q):
                for t in range(2):
                    b = 2 * j + t
                    if due(b - 1):
                        pe.wait_ge(s["gated2_ready"], b - 1)
                    for c in range(FC):
                        n = 128 if c < FC - 1 else FL + 1
                        if t == 0:
                            pe.wait_ge(s["silu_done"], FC * j + c + 1)
                        last = mmul(bank[5 + t][:, 0:D], hT[q][0:n, c, t * 128:(t + 1) * 128], w2[0:n, c, :],
                                    start=(c == 0), stop=(c == FC - 1))
                    last.then_inc(s["w2_done"], 1)

            def pair(j, q, front):
                expand(j, q)
                if front:
                    front_x2(j + 1)
                contract(j, q)

            front_x2(0)
            pair(0, 0, True)
            with pe.Fori(0, (NPAIR - 2) // 2) as k:
                pair(2 * k + 1, 1, True)
                pair(2 * k + 2, 0, True)
            pair(NPAIR - 1, 1, False)


_INS = ['x', 'cond_1152', 'L0_cond_Wq', 'L0_cond_Wk', 'L0_cond_Wv', 'L0_cond_Wp', 'L0_cond_bp', 'L0_cond_W1',
        'L0_cond_b1', 'L0_cond_W2', 'L0_cond_b2', 'L0_cond_Wa', 'L0_cond_ba']


def kernel(**inputs):
    import numpy as _np
    import concourse.bacc as _bacc
    from concourse import mybir as _mybir
    from concourse.bass_utils import run_bass_kernel_spmd as _run

    nc = _bacc.Bacc("TRN2", target_bir_lowering=False, num_devices=1)
    arrays, args = {}, []
    for name in _INS:
        a = _np.ascontiguousarray(inputs[name])
        arrays[f"in_{name}"] = a
        args.append(nc.dram_tensor(f"in_{name}", a.shape, _mybir.dt.from_np(a.dtype), kind="ExternalInput").ap())
    out = nc.dram_tensor("out", (NB, T, D), F32, kind="ExternalOutput").ap()
    build(nc, *args, out)
    r = _run(nc, [arrays], core_ids=[0])
    return r.results[0]["out"]
```

```python
from contextlib import ExitStack

import numpy as np

import concourse.bass as bass
from concourse import mybir

F32 = mybir.dt.float32
F32R = mybir.dt.float32r
BF16 = mybir.dt.bfloat16
ALU = mybir.AluOpType
ACT = mybir.ActivationFunctionType
AX = mybir.AxisListType

NB, T, D = 32, 128, 144
H = 16
HD = D // H
FF = 4 * D
EPS = 1e-6
SCALE = float(1.0 / np.sqrt(HD))
KA = 128
KB = D - KA
HH = H // 2
FC = (FF + 127) // 128
FL = FF - (FC - 1) * 128
MASKED = -3.0e38
Y_LO_B, Y_HI_B, Y_LO_A = D, D + KB, D + 2 * KB
YW = D + 2 * KB + KA
HS = 64


def slots(q, k):
    return q * HD, H * HS + (k - q) * HD


def build(nc, x, cond, Wq, Wk, Wv, Wp, bp, W1, b1, W2, b2, Wa, ba, out):
    mod_dram = nc.dram_tensor("modulation", [NB, 6 * D], F32, kind="Internal").ap()
    ctx = ExitStack()
    with ctx:
        def sb(name, shape, dt=F32):
            return ctx.enter_context(nc.sbuf_tensor(name, shape, dt))

        def sem(name):
            return ctx.enter_context(nc.semaphore(name))

        def view(t, offset, dims, parts=128):
            width = int(np.prod(t.shape[1:]))
            return bass.AP(t, offset, [[width, parts], *dims])

        def slot_pair(p, q, k):
            offset, step = slots(q, k)
            return view(stack[p], offset, [[step, 2], [HS, H], [1, HD]])

        identf = sb("identf", [128, 128])
        identb = sb("identb", [128, 128], BF16)
        mask = sb("mask", [128, 128], BF16)
        pick = sb("pick", [128, HH, 128], BF16)
        wqkv = sb("wqkv", [128, 3 * D])
        wqkv_tail = sb("wqkv_tail", [3 * KB, 3 * D])
        w1 = sb("w1", [128, FF])
        w1_tail = sb("w1_tail", [3 * KB, FF])
        wqkv_hi = sb("wqkv_hi", [128, 3 * D], F32R)
        wqkv_lo = sb("wqkv_lo", [128, 3 * D], F32R)
        wqkv_rest = sb("wqkv_rest", [3 * KB, 3 * D], F32R)
        w1_hi = sb("w1_hi", [128, FF], F32R)
        w1_lo = sb("w1_lo", [128, FF], F32R)
        w1_rest = sb("w1_rest", [3 * KB, FF], F32R)
        wp_a = sb("wp_a", [128, D])
        wp_b = sb("wp_b", [KB + 1, D])
        w2 = sb("w2", [128, FC, D])
        b1c = sb("b1c", [128, FC])
        wa_a = sb("wa_a", [128, 6 * D])
        wa_b = sb("wa_b", [KB + 1, 6 * D])
        cond_sb = sb("cond_sb", [NB, D])
        cond_silu = sb("cond_silu", [NB, D + 1])
        condT = sb("condT", [128, 2, NB])
        mod = sb("mod", [NB, 6 * D])
        xr = sb("xr", [128, NB, D])
        st1 = sb("st1", [128, NB, 6])
        st2 = sb("st2", [128, NB, 6])
        mean_gap = sb("mean_gap", [128, NB])
        mean_sum = sb("mean_sum", [128, NB])
        within = sb("within", [128, NB])
        across = sb("across", [128, NB])
        ve = sb("ve", [128, NB])
        sd = sb("sd", [128, NB])
        rsd = sb("rsd", [128, NB])
        rstd = sb("rstd", [128, NB])
        nmr = sb("nmr", [128, NB])
        bcm = [sb(f"bcm{p}", [128, 2 * D]) for p in range(2)]
        bcg = [sb(f"bcg{p}", [128, D]) for p in range(2)]
        tn = [sb(f"tn{p}", [128, D]) for p in range(2)]
        ts = [sb(f"ts{p}", [128, D]) for p in range(2)]
        ym = [sb(f"ym{p}", [128, D]) for p in range(2)]
        y3 = [sb(f"y3{p}", [128, YW], F32R) for p in range(2)]
        yT = [sb(f"yT{p}", [128, 3, 256], F32R) for p in range(2)]
        stack = [sb(f"stack{p}", [128, 2 * H * HS], BF16) for p in range(2)]
        resid = [sb(f"resid{p}", [128, 2 * D]) for p in range(2)]
        vx = [sb(f"vx{p}", [128, H, HD + 1]) for p in range(2)]
        qkT = [sb(f"qkT{p}", [128, 2, HH, 128], BF16) for p in range(2)]
        mx = sb("mx", [128, 2, HH])
        mm = [sb(f"mm{h}", [128, 128], BF16) for h in range(2)]
        mT = [sb(f"mT{h}", [128, 128], BF16) for h in range(2)]
        P = [sb(f"P{h}", [128, HH, 128]) for h in range(2)]
        ctxT = sb("ctxT", [128, 4, 128])
        rden = sb("rden", [128, H])
        ctxn = sb("ctxn", [128, D + 1])
        backT = sb("backT", [128, 2, 128])
        gated = sb("gated", [128, D])
        hT = [sb(f"hT{p}", [128, FC, 256]) for p in range(2)]
        gated2 = [sb(f"gated2{t}", [128, D]) for t in range(2)]

        bank = [ctx.enter_context(nc.psum_tensor(f"bank{i}", [128, 512], F32)) for i in range(8)]
        B_XT, B_QKV, B_QKT, B_CTX = 0, 1, 2, 7
        S_BANK = (3, 4)
        ST_BANK = (5, 6)
        H_BANK = (2, 3, 4, 2, 3)

        s = {n: sem(n) for n in (
            "x_in0 x_in1 x_in2 x_in3 cond_in wa_in wqkv_in w1_in wp_in w2_in b1_in "
            "mod_out0 mod_out1 bcm_in0 bcm_in1 bcg_in0 bcg_in1 out_done "
            "identities consts vconsts cond_act cond_T condT_ev mod_mm mod_ev weights "
            "stats moments ve_ready sd_ready nchain norm_ready "
            "t_ready scaled ym_ready yhi_ready y_ready xT_done yT_ready qkv_done v_ready resid_ready "
            "mid_ready stack_ready dup_ready qT_done kT_done qTev kTev "
            "s_done max_done mhi mm_ready mT_done mT_ev st_done exp_done p_ready pv_done "
            "ctxT_ev tok_done rden_ready ctxn_ready back_done back_ev wp_done gated_read x1_ready stats2 "
            "bc2_in0 bc2_in1 t2_ready scaled2 ym2_ready yhi2_ready y2_ready xT2_done yT2_ready w1_done silu_done w2_done "
            "gated2_ready result_ready").split()}

        def due(count):
            return not (isinstance(count, int) and count <= 0)

        def later(i, p, d):
            return i + (p + d) // 2, (p + d) % 2

        def sequences(eng, step):
            step(0, 0, False, 3)
            step(0, 1, True, 3)
            step(1, 0, True, 3)
            with eng.Fori(1, (NB - 4) // 2) as i:
                step(i, 1, True, 3)
                step(i + 1, 0, True, 3)
            for b in range(NB - 3, NB):
                step(b // 2, b % 2, True, NB - 1 - b)

        XG = NB // 4
        NEARLY = NB - 4
        NPAIR = NB // 2
        block = ctx.enter_context(nc.Block())

        @block.sync
        def _(sp):
            xv = x.rearrange("b t d -> t b d")

            def load_x(g):
                sp.dma_start(xr[:, g * XG:(g + 1) * XG, :], xv[:, g * XG:(g + 1) * XG, :])\
                    .then_inc(s[f"x_in{g}"], 16)

            sp.dma_start(cond_sb[:, :], cond).then_inc(s["cond_in"], 16)
            load_x(0)
            sp.dma_start(wa_a[:, :], Wa[0:KA, :]).then_inc(s["wa_in"], 16)
            sp.dma_start(wa_b[0:KB, :], Wa[KA:D, :]).then_inc(s["wa_in"], 16)
            sp.dma_start(wa_b[KB:KB + 1, :], ba.unsqueeze(0)).then_inc(s["wa_in"], 16)
            for g in range(1, 4):
                load_x(g)
            for n, w in enumerate((Wq, Wk, Wv)):
                sp.dma_start(wqkv[:, n * D:(n + 1) * D], w[0:KA, :]).then_inc(s["wqkv_in"], 16)
                for r in range(3):
                    sp.dma_start(wqkv_tail[r * KB:(r + 1) * KB, n * D:(n + 1) * D], w[KA:D, :])\
                        .then_inc(s["wqkv_in"], 16)
            sp.dma_start(wp_a[:, :], Wp[0:KA, :]).then_inc(s["wp_in"], 16)
            sp.dma_start(wp_b[0:KB, :], Wp[KA:D, :]).then_inc(s["wp_in"], 16)
            sp.dma_start(wp_b[KB:KB + 1, :], bp.unsqueeze(0)).then_inc(s["wp_in"], 16)
            sp.dma_start(w1[:, :], W1[0:KA, :]).then_inc(s["w1_in"], 16)
            for r in range(3):
                sp.dma_start(w1_tail[r * KB:(r + 1) * KB, :], W1[KA:D, :]).then_inc(s["w1_in"], 16)
            sp.dma_start(w2[:, 0:FC - 1, :], W2[0:(FC - 1) * 128, :].rearrange("(c p) d -> p c d", p=128))\
                .then_inc(s["w2_in"], 16)
            sp.dma_start(w2[0:FL, FC - 1, :], W2[(FC - 1) * 128:FF, :]).then_inc(s["w2_in"], 16)
            sp.dma_start(w2[FL:FL + 1, FC - 1, :], b2.unsqueeze(0)).then_inc(s["w2_in"], 16)
            with nc.allow_non_contiguous_dma(reason="the bias of the hidden layer, one element a partition"):
                sp.dma_start(b1c[:, 0:FC - 1], b1[0:(FC - 1) * 128].rearrange("(c p) -> p c", p=128))\
                    .then_inc(s["b1_in"], 16)
                sp.dma_start(b1c[0:FL, FC - 1:FC], b1[(FC - 1) * 128:FF].unsqueeze(1)).then_inc(s["b1_in"], 16)
            for n in range(2):
                half = slice(n * 3 * D, (n + 1) * 3 * D)
                sp.wait_ge(s["mod_ev"], 2 * n + 2)
                sp.dma_start(mod_dram[:, half], mod[:, half]).then_inc(s[f"mod_out{n}"], 16)
            sp.wait_ge(s["mod_out0"], 16)

            def row(b, lo, n):
                return mod_dram[bass.ds(b, 1), lo:lo + n].to_broadcast([128, n]) if not isinstance(b, int) \
                    else mod_dram[b:b + 1, lo:lo + n].to_broadcast([128, n])

            def load_modulation(i, p):
                b = 2 * i + p
                if due(b - 1):
                    sp.wait_ge(s["ym_ready"], b - 1)
                sp.dma_start(bcm[p][:, :], row(b, 0, 2 * D)).then_inc(s[f"bcm_in{p}"], 16)

            def step(i, p, tail, more):
                b = 2 * i + p
                if more >= 2:
                    load_modulation(*later(i, p, 2))
                if due(b - 1):
                    sp.wait_ge(s["gated_read"], b - 1)
                sp.dma_start(bcg[p][:, :], row(b, 2 * D, D)).then_inc(s[f"bcg_in{p}"], 16)

            load_modulation(0, 0)
            load_modulation(0, 1)
            sequences(sp, step)

            def load2(j, t):
                b = 2 * j + t
                if due(b - 1):
                    sp.wait_ge(s["ym2_ready"], b - 1)
                sp.dma_start(bcm[t][:, :], row(b, 3 * D, 2 * D)).then_inc(s[f"bc2_in{t}"], 16)

            def gate2(j, t):
                b = 2 * j + t
                if due(b - 1):
                    sp.wait_ge(s["gated2_ready"], b - 1)
                sp.dma_start(bcg[t][:, :], row(b, 5 * D, D)).then_inc(s[f"bcg_in{t}"], 16)

            sp.wait_ge(s["mod_out1"], 16)
            sp.wait_ge(s["ym_ready"], NB)
            load2(0, 0)
            load2(0, 1)

            def pair2(j, last):
                if not last:
                    load2(j + 1, 0)
                    load2(j + 1, 1)
                gate2(j, 0)
                gate2(j, 1)

            load2(1, 0)
            load2(1, 1)
            sp.wait_ge(s["gated_read"], NB)
            gate2(0, 0)
            gate2(0, 1)
            with sp.Fori(1, NPAIR - 1) as j:
                pair2(j, False)
                sp.wait_ge(s["result_ready"], 2 * j)
                sp.dma_start(out.rearrange("b t d -> t b d")[:, bass.ds(2 * j - 2, 2), :],
                             xr[:, bass.ds(2 * j - 2, 2), :]).then_inc(s["out_done"], 16)
            pair2(NPAIR - 1, True)
            for j in (NPAIR - 2, NPAIR - 1):
                sp.wait_ge(s["result_ready"], 2 * j + 2)
                sp.dma_start(out.rearrange("b t d -> t b d")[:, 2 * j:2 * j + 2, :],
                             xr[:, 2 * j:2 * j + 2, :]).then_inc(s["out_done"], 16)
            sp.wait_ge(s["out_done"], 16 * NPAIR)

        @block.gpsimd
        def _(pool):
            g = nc.gpsimd
            g.memset(identf[:, :], 0.0)
            g.memset(identb[:, :], 0.0).then_inc(s["identities"], 1)
            pool.wait_ge(s["identities"], 1)
            for m in (identf, identb):
                last = g.affine_select(out=m[:, :], in_=m[:, :], compare_op=ALU.not_equal, fill=1.0, base=0,
                                       pattern=[[-1, 128]], channel_multiplier=1)
            last.then_inc(s["identities"], 1)
            g.memset(mask[:, :], 0.0)
            g.memset(pick[:, :, :], 0.0)
            g.memset(mm[0][:, :], 0.0)
            g.memset(mm[1][:, :], 0.0)
            g.memset(ctxn[:, D:D + 1], 1.0)
            g.memset(vx[0][:, :, :], 1.0)
            g.memset(vx[1][:, :, :], 1.0).then_inc(s["consts"], 1)
            pool.wait_ge(s["consts"], 1)
            g.affine_select(out=mask[:, :], in_=mask[:, :], compare_op=ALU.is_ge, fill=MASKED, base=0,
                            pattern=[[-1, 128]], channel_multiplier=1)
            g.affine_select(out=pick[:, :, :], in_=pick[:, :, :], compare_op=ALU.not_equal, fill=-1.0,
                            base=0, pattern=[[-1, HH], [0, 128]], channel_multiplier=1)\
                .then_inc(s["consts"], 1)
            pool.wait_ge(s["consts"], 2)
            g.affine_select(out=pick[:, :, :], in_=pick[:, :, :], compare_op=ALU.not_equal, fill=-1.0,
                            base=-HH, pattern=[[-1, HH], [0, 128]], channel_multiplier=1)\
                .then_inc(s["consts"], 1)

            def standing():
                pool.nop(nofuse=True)

            def modulate(b, p, ready, arrived, count, scaled, ym_ready, yhi, y_ready, used, used_count):
                pool.wait_ge(s[arrived], count)
                pool.wait_ge(s[ready], b + 1)
                g.tensor_tensor(ts[p][:, :], tn[p][:, :], bcm[p][:, D:2 * D], ALU.mult).then_inc(s[scaled], 1)
                pool.wait_ge(s[scaled], b + 1)
                g.tensor_tensor(ym[p][:, :], ts[p][:, :], bcm[p][:, 0:D], ALU.add).then_inc(s[ym_ready], 1)
                pool.wait_ge(s[ym_ready], b + 1)
                if due(used_count):
                    pool.wait_ge(s[used], used_count)
                standing()
                g.tensor_scalar(y3[p][:, 0:D], ym[p][:, :], 1.0, 0.0, ALU.mult, ALU.add).then_inc(s[yhi], 1)
                g.tensor_scalar(y3[p][:, Y_HI_B:Y_HI_B + KB], ym[p][:, KA:D], 1.0, 0.0, ALU.mult, ALU.add)
                pool.wait_ge(s[yhi], b + 1)
                g.tensor_tensor(y3[p][:, Y_LO_B:Y_LO_B + KB], ym[p][:, KA:D], y3[p][:, KA:D].bitcast(F32),
                                ALU.subtract)
                g.tensor_tensor(y3[p][:, Y_LO_A:YW], ym[p][:, 0:KA], y3[p][:, 0:KA].bitcast(F32), ALU.subtract)\
                    .then_inc(s[y_ready], 1)

            def modulate1(i, p):
                b = 2 * i + p
                modulate(b, p, "t_ready", f"bcm_in{p}", 16 * i + 16, "scaled", "ym_ready", "yhi_ready", "y_ready",
                         "xT_done", b - 1)

            def split(i, p):
                b = 2 * i + p
                pool.wait_ge(s["resid_ready"], b + 1)
                standing()
                r = view(resid[p], 0, [[D, 2], [HD, H], [1, HD]])
                mid = slot_pair(p, 2, 2)
                g.tensor_scalar(mid, r, 1.0, 0.0, ALU.mult, ALU.add).then_inc(s["mid_ready"], 1)
                g.tensor_scalar(slot_pair(p, 3, 1), r, 1.0, 0.0, ALU.mult, ALU.add)
                pool.wait_ge(s["mid_ready"], b + 1)
                g.tensor_tensor(slot_pair(p, 5, 4), r, mid, ALU.subtract).then_inc(s["stack_ready"], 1)

            def select(i, p, h):
                b = 2 * i + p
                pool.wait_ge(s["exp_done"], 2 * b + h + 1)
                standing()
                g.affine_select(out=P[h][:, :, :], in_=P[h][:, :, :], compare_op=ALU.is_ge, fill=0.0,
                                base=0, pattern=[[0, HH], [1, 128]], channel_multiplier=-1)\
                    .then_inc(s["p_ready"], 1)

            modulate1(0, 0)
            modulate1(0, 1)
            split(0, 0)

            def step(i, p, tail, more):
                if tail:
                    select(*later(i, p, -1), 1)
                if more >= 2:
                    modulate1(*later(i, p, 2))
                if more >= 1:
                    split(*later(i, p, 1))
                else:
                    modulate2(0)
                select(i, p, 0)

            def modulate2(j):
                for t in range(2):
                    b = 2 * j + t
                    modulate(b, t, "t2_ready", f"bc2_in{t}", 16 * j + 16, "scaled2", "ym2_ready", "yhi2_ready",
                             "y2_ready", "xT2_done", b - 1)

            sequences(pool, step)
            select(NPAIR - 1, 1, 1)
            with pool.Fori(1, NPAIR) as j:
                modulate2(j)

        @block.scalar
        def _(act):
            a = nc.scalar
            act.wait_ge(s["vconsts"], 1)
            act.wait_ge(s["cond_in"], 16)
            a.activation(cond_silu[:, 0:D], cond_sb[:, :], ACT.Silu).then_inc(s["cond_act"], 1)
            act.wait_ge(s["cond_T"], 1)
            a.copy(condT[:, 0, :], bank[0][:, 0:NB])
            a.copy(condT[0:KB + 1, 1, :], bank[0][0:KB + 1, NB:2 * NB]).then_inc(s["condT_ev"], 1)
            for n in range(2):
                dst = mod[:, n * 3 * D:(n + 1) * 3 * D].rearrange("p (n d) -> p n d", n=3)
                src = bank[1 + n][0:NB, 0:3 * D].rearrange("p (n d) -> p n d", n=3)
                act.wait_ge(s["mod_mm"], n + 1)
                a.copy(dst[:, 0:3:2, :], src[:, 0:3:2, :]).then_inc(s["mod_ev"], 1)
                a.add(dst[:, 1, :], src[:, 1, :], 1.0).then_inc(s["mod_ev"], 1)

            def deviation(times, lo, hi):
                act.wait_ge(s["ve_ready"], times)
                a.activation(sd[:, lo:hi], ve[:, lo:hi], ACT.Sqrt).then_inc(s["sd_ready"], 1)

            deviation(1, 0, NB)

            def evacuate_y(i, p):
                b = 2 * i + p
                act.wait_ge(s["xT_done"], b + 1)
                a.copy(yT[p][:, 0:2, 0:128], bank[B_XT][:, 0:256].rearrange("p (c t) -> p c t", c=2))
                a.copy(yT[p][0:3 * KB, 2, 0:128], bank[B_XT][0:3 * KB, 256:384]).then_inc(s["yT_ready"], 1)

            def evacuate_qkv(i, p):
                b = 2 * i + p
                act.wait_ge(s["qkv_done"], b + 1)
                if due(b - 1):
                    act.wait_ge(s["kT_done"], b - 1)
                a.copy(slot_pair(p, 0, 0),
                       bank[B_QKV][:, 0:2 * D].rearrange("p (w h d) -> p w h d", w=2, h=H))
                if due(2 * b - 2):
                    act.wait_ge(s["pv_done"], 2 * b - 2)
                a.copy(vx[p][:, :, 0:HD], bank[B_QKV][:, 2 * D:3 * D].rearrange("p (h d) -> p h d", h=H))\
                    .then_inc(s["v_ready"], 1)

            def evacuate_mT(i, p, h):
                b = 2 * i + p
                act.wait_ge(s["mT_done"], 2 * b + h + 1)
                if due(2 * b + h - 1):
                    act.wait_ge(s["st_done"], 2 * b + h - 1)
                a.copy(mT[h][:, :], bank[B_QKV][:, 448:512].bitcast(BF16)).then_inc(s["mT_ev"], 1)

            def exponentials(i, p, h, n):
                b = 2 * i + p
                if n == 0:
                    act.wait_ge(s["st_done"], 2 * b + h + 1)
                    if due(2 * b + h - 1):
                        act.wait_ge(s["pv_done"], 2 * b + h - 1)
                last = a.activation(P[h][:, n * HH // 2:(n + 1) * HH // 2, :],
                                    bank[ST_BANK[n]][:, :].rearrange("p (h t) -> p h t", t=128), ACT.Exp,
                                    scale=SCALE)
                if n == 1:
                    last.then_inc(s["exp_done"], 1)

            def evacuate_ctx(i, p):
                b = 2 * i + p
                act.wait_ge(s["pv_done"], 2 * b + 2)
                if due(b):
                    act.wait_ge(s["tok_done"], b)
                a.copy(ctxT[:, :, :], bank[B_CTX][:, :].rearrange("p (g t) -> p g t", t=128))\
                    .then_inc(s["ctxT_ev"], 1)

            def evacuate_back(i, p):
                b = 2 * i + p
                act.wait_ge(s["back_done"], b + 1)
                if due(b):
                    act.wait_ge(s["wp_done"], b)
                a.copy(backT[:, 0, :], bank[B_CTX][:, 0:128])
                a.copy(backT[0:KB + 1, 1, :], bank[B_CTX][0:KB + 1, 128:256]).then_inc(s["back_ev"], 1)

            evacuate_y(0, 0)
            evacuate_y(0, 1)
            evacuate_qkv(0, 0)

            def step(i, p, tail, more):
                if tail and more == 1:
                    deviation(2, 0, NEARLY)
                if tail:
                    evacuate_ctx(*later(i, p, -1))
                if more >= 1:
                    evacuate_qkv(*later(i, p, 1))
                evacuate_mT(i, p, 0)
                exponentials(i, p, 0, 0)
                evacuate_mT(i, p, 1)
                exponentials(i, p, 0, 1)
                if more >= 2:
                    evacuate_y(*later(i, p, 2))
                if tail:
                    evacuate_back(*later(i, p, -1))
                exponentials(i, p, 1, 0)
                exponentials(i, p, 1, 1)

            sequences(act, step)
            evacuate_ctx(NPAIR - 1, 1)
            evacuate_back(NPAIR - 1, 1)

            act.wait_ge(s["b1_in"], 32)

            def hidden(j, q):
                for c in range(FC):
                    n = 128 if c < FC - 1 else FL
                    act.wait_ge(s["w1_done"], FC * j + c + 1)
                    if c == 0:
                        if due(2 * j - 2):
                            act.wait_ge(s["w2_done"], 2 * j - 2)
                    a.activation(hT[q][0:n, c, :], bank[H_BANK[c]][0:n, 0:256], ACT.Silu,
                                 bias=b1c[0:n, c:c + 1]).then_inc(s["silu_done"], 1)

            hidden(0, 0)
            deviation(3, NEARLY, NB)
            hidden(1, 1)
            with act.Fori(1, NPAIR // 2) as k:
                hidden(2 * k, 0)
                hidden(2 * k + 1, 1)

        @block.vector
        def _(dve):
            v = nc.vector
            v.memset(cond_silu[:, D:D + 1], 1.0)
            for q in range(2):
                v.memset(hT[q][FL:FL + 1, FC - 1, :], 1.0)
            for p in range(2):
                v.memset(view(stack[p], 6 * HD, [[HS, 2 * H], [1, HS - 6 * HD]]), 0.0)
            v.memset(bank[B_CTX][:, :], 0.0).then_inc(s["vconsts"], 1)
            for n in range(4):
                dve.wait_ge(s[f"x_in{n}"], 16)
                for b in range(n * XG, (n + 1) * XG):
                    last = v.bn_stats(st1[:, b, :], xr[:, b, :])
            last.then_inc(s["stats"], 1)
            dve.wait_ge(s["stats"], 1)

            def moments(times, st, lo, hi):
                g = slice(lo, hi)
                v.tensor_tensor(mean_gap[:, g], st[:, g, 1], st[:, g, 4], ALU.subtract)
                v.tensor_tensor(mean_sum[:, g], st[:, g, 1], st[:, g, 4], ALU.add)
                v.tensor_tensor(within[:, g], st[:, g, 2], st[:, g, 5], ALU.add).then_inc(s["moments"], 1)
                dve.wait_ge(s["moments"], 2 * times - 1)
                v.scalar_tensor_tensor(out=across[:, g], in0=mean_gap[:, g], scalar=0.25, in1=mean_gap[:, g],
                                       op0=ALU.mult, op1=ALU.mult)
                v.tensor_scalar(within[:, g], within[:, g], 1.0 / D, EPS, ALU.mult, ALU.add)\
                    .then_inc(s["moments"], 1)
                dve.wait_ge(s["moments"], 2 * times)
                v.tensor_tensor(ve[:, g], within[:, g], across[:, g], ALU.add).then_inc(s["ve_ready"], 1)

            def inverse_deviation(times, lo, hi):
                g = slice(lo, hi)
                base = 4 * (times - 1)
                dve.wait_ge(s["sd_ready"], times)
                v.reciprocal(rsd[:, g], sd[:, g]).then_inc(s["nchain"], 1)
                dve.wait_ge(s["nchain"], base + 1)
                v.tensor_tensor(rsd[:, g], rsd[:, g], ve[:, g], ALU.mult).then_inc(s["nchain"], 1)
                dve.wait_ge(s["nchain"], base + 2)
                v.tensor_tensor(rsd[:, g], rsd[:, g], sd[:, g], ALU.add).then_inc(s["nchain"], 1)
                dve.wait_ge(s["nchain"], base + 3)
                v.reciprocal(rstd[:, g], rsd[:, g]).then_inc(s["nchain"], 1)
                dve.wait_ge(s["nchain"], base + 4)
                v.tensor_scalar(rstd[:, g], rstd[:, g], 2.0, None, ALU.mult).then_inc(s["norm_ready"], 1)
                dve.wait_ge(s["norm_ready"], 2 * times - 1)
                v.scalar_tensor_tensor(out=nmr[:, g], in0=mean_sum[:, g], scalar=-0.5, in1=rstd[:, g],
                                       op0=ALU.mult, op1=ALU.mult).then_inc(s["norm_ready"], 1)
                dve.wait_ge(s["norm_ready"], 2 * times)

            moments(1, st1, 0, NB)
            dve.wait_ge(s["wqkv_in"], 12 * 16)
            v.tensor_copy(wqkv_hi[:, :], wqkv[:, :])
            v.tensor_copy(wqkv_rest[:, :], wqkv_tail[:, :]).then_inc(s["weights"], 1)
            dve.wait_ge(s["weights"], 1)
            v.tensor_tensor(wqkv_lo[:, :], wqkv[:, :], wqkv_hi[:, :].bitcast(F32), ALU.subtract)
            v.tensor_tensor(wqkv_rest[2 * KB:3 * KB, :], wqkv_tail[2 * KB:3 * KB, :],
                            wqkv_rest[2 * KB:3 * KB, :].bitcast(F32), ALU.subtract).then_inc(s["weights"], 1)
            inverse_deviation(1, 0, NB)

            def normalize(b, p, name, used):
                if due(b - 1):
                    dve.wait_ge(s[used], b - 1)
                v.tensor_scalar(tn[p][:, :], xr[:, b, :] if isinstance(b, int) else xr[:, bass.ds(b, 1), :],
                                rstd[:, bass.ds(b, 1)], nmr[:, bass.ds(b, 1)], ALU.mult, ALU.add)\
                    .then_inc(s[name], 1)

            def residuals(i, p):
                b = 2 * i + p
                dve.wait_ge(s["v_ready"], b + 1)
                if due(b - 1):
                    dve.wait_ge(s["stack_ready"], b - 1)
                hi = slot_pair(p, 0, 0)
                v.tensor_tensor(resid[p][:, :].rearrange("p (w h d) -> p w h d", w=2, h=H),
                                bank[B_QKV][:, 0:2 * D].rearrange("p (w h d) -> p w h d", w=2, h=H),
                                hi, ALU.subtract).then_inc(s["resid_ready"], 1)

            def copies(i, p):
                hi = slot_pair(p, 0, 0)
                v.tensor_copy(slot_pair(p, 1, 3), hi)
                v.tensor_copy(slot_pair(p, 4, 5), hi).then_inc(s["dup_ready"], 1)

            def maxima(i, p, h):
                b = 2 * i + p
                dve.wait_ge(s["s_done"], 2 * b + h + 1)
                for n, k in enumerate(S_BANK):
                    last = v.tensor_reduce(mx[:, h, n * HH // 2:(n + 1) * HH // 2],
                                           bank[k][:, :].rearrange("p (h t) -> p h t", t=128), AX.X, ALU.max)
                last.then_inc(s["max_done"], 1)
                dve.wait_ge(s["max_done"], 2 * b + h + 1)
                if due(2 * b + h - 1):
                    dve.wait_ge(s["mT_done"], 2 * b + h - 1)
                v.tensor_copy(mm[h][:, 0:HH], mx[:, h, :]).then_inc(s["mhi"], 1)
                dve.wait_ge(s["mhi"], 2 * b + h + 1)
                v.tensor_tensor(mm[h][:, HH:2 * HH], mx[:, h, :], mm[h][:, 0:HH], ALU.subtract)\
                    .then_inc(s["mm_ready"], 1)

            def evacuate_T(i, p, w):
                b = 2 * i + p
                dve.wait_ge(s[("qT_done", "kT_done")[w]], b + 1)
                if due(2 * b - 2):
                    dve.wait_ge(s["st_done"], 2 * b - 2)
                v.tensor_copy(qkT[p][:, w, :, :], bank[B_QKT][:, :].bitcast(BF16)
                              .rearrange("p (j t) -> p j t", t=128)).then_inc(s[("qTev", "kTev")[w]], 1)

            def divide(i, p):
                b = 2 * i + p
                tok = bank[B_CTX][:, :].rearrange("p (h c) -> p h c", c=32)
                dve.wait_ge(s["tok_done"], b + 1)
                v.reciprocal(rden[:, :], tok[:, :, HD]).then_inc(s["rden_ready"], 1)
                dve.wait_ge(s["rden_ready"], b + 1)
                if due(b):
                    dve.wait_ge(s["back_done"], b)
                v.tensor_tensor(ctxn[:, 0:D].rearrange("p (h d) -> p h d", d=HD), tok[:, :, 0:HD],
                                rden[:, :].unsqueeze(2).to_broadcast([128, H, HD]), ALU.mult)\
                    .then_inc(s["ctxn_ready"], 1)

            def gate_attention(i, p):
                b = 2 * i + p
                dve.wait_ge(s["wp_done"], b + 1)
                dve.wait_ge(s[f"bcg_in{p}"], 16 * i + 16)
                v.tensor_tensor(gated[:, :], bank[B_CTX][:, 0:D], bcg[p][:, :], ALU.mult)\
                    .then_inc(s["gated_read"], 1)

            def add_attention(i, p):
                b = 2 * i + p
                dve.wait_ge(s["gated_read"], b + 1)
                row = xr[:, bass.ds(b, 1), :]
                v.tensor_tensor(row, row, gated[:, :].unsqueeze(1), ALU.add).then_inc(s["x1_ready"], 1)

            def statistics(i, p):
                b = 2 * i + p
                dve.wait_ge(s["x1_ready"], b + 1)
                v.bn_stats(st2[:, bass.ds(b, 1), :], xr[:, bass.ds(b, 1), :]).then_inc(s["stats2"], 1)

            normalize(0, 0, "t_ready", "scaled")
            normalize(1, 1, "t_ready", "scaled")
            normalize(2, 0, "t_ready", "scaled")
            dve.wait_ge(s["w1_in"], 4 * 16)
            v.tensor_copy(w1_hi[:, :], w1[:, :])
            v.tensor_copy(w1_rest[:, :], w1_tail[:, :]).then_inc(s["weights"], 1)
            dve.wait_ge(s["weights"], 3)
            v.tensor_tensor(w1_lo[:, :], w1[:, :], w1_hi[:, :].bitcast(F32), ALU.subtract)
            v.tensor_tensor(w1_rest[2 * KB:3 * KB, :], w1_tail[2 * KB:3 * KB, :],
                            w1_rest[2 * KB:3 * KB, :].bitcast(F32), ALU.subtract).then_inc(s["weights"], 1)
            residuals(0, 0)
            copies(0, 0)
            evacuate_T(0, 0, 0)
            evacuate_T(0, 0, 1)

            def normalize2(j):
                for t in range(2):
                    normalize(2 * j + t, t, "t2_ready", "scaled2")

            def evacuate_y2(j, q):
                for t in range(2):
                    b = 2 * j + t
                    dve.wait_ge(s["xT2_done"], b + 1)
                    if t == 0:
                        if due(FC * j - FC):
                            dve.wait_ge(s["w1_done"], FC * j - FC)
                    v.tensor_copy(yT[q][:, 0:2, t * 128:(t + 1) * 128],
                                  bank[t][:, 0:256].rearrange("p (c t) -> p c t", c=2))
                    v.tensor_copy(yT[q][0:3 * KB, 2, t * 128:(t + 1) * 128], bank[t][0:3 * KB, 256:384])\
                        .then_inc(s["yT2_ready"], 1)

            def step(i, p, tail, more):
                maxima(i, p, 0)
                if more >= 1:
                    residuals(*later(i, p, 1))
                maxima(i, p, 1)
                if more >= 1:
                    copies(*later(i, p, 1))
                if tail:
                    divide(*later(i, p, -1))
                if more >= 1:
                    evacuate_T(*later(i, p, 1), 0)
                if tail:
                    gate_attention(*later(i, p, -1))
                if more >= 1:
                    evacuate_T(*later(i, p, 1), 1)
                if tail:
                    add_attention(*later(i, p, -1))
                if more >= 3:
                    ia, pa = later(i, p, 3)
                    normalize(2 * ia + pa, pa, "t_ready", "scaled")
                if tail:
                    statistics(*later(i, p, -1))
                if tail and more == 2:
                    dve.wait_ge(s["stats2"], NEARLY)
                    moments(2, st2, 0, NEARLY)
                if tail and more == 1:
                    inverse_deviation(2, 0, NEARLY)
                    normalize2(0)

            sequences(dve, step)
            evacuate_y2(0, 0)
            divide(NPAIR - 1, 1)
            gate_attention(NPAIR - 1, 1)
            add_attention(NPAIR - 1, 1)
            normalize2(1)
            statistics(NPAIR - 1, 1)
            dve.wait_ge(s["stats2"], NB)
            moments(3, st2, NEARLY, NB)

            def add_mlp(j):
                for t in range(2):
                    b = 2 * j + t
                    dve.wait_ge(s["w2_done"], b + 1)
                    dve.wait_ge(s[f"bcg_in{t}"], 16 * (NPAIR + 1) + 16 * j)
                    if due(b - 1):
                        dve.wait_ge(s["result_ready"], b - 1)
                    v.tensor_tensor(gated2[t][:, :], bank[5 + t][:, 0:D], bcg[t][:, :], ALU.mult)\
                        .then_inc(s["gated2_ready"], 1)
                for t in range(2):
                    b = 2 * j + t
                    dve.wait_ge(s["gated2_ready"], b + 1)
                    row = xr[:, bass.ds(b, 1), :]
                    v.tensor_tensor(row, row, gated2[t][:, :].unsqueeze(1), ALU.add).then_inc(s["result_ready"], 1)

            def pair(j, q, front, ahead):
                if ahead:
                    normalize2(j + 2)
                if front:
                    evacuate_y2(j + 1, 1 - q)
                add_mlp(j)

            pair(0, 0, True, True)
            inverse_deviation(3, NEARLY, NB)
            with dve.Fori(0, (NPAIR - 4) // 2) as k:
                pair(2 * k + 1, 1, True, True)
                pair(2 * k + 2, 0, True, True)
            pair(NPAIR - 3, 1, True, True)
            pair(NPAIR - 2, 0, True, False)
            pair(NPAIR - 1, 1, False, False)

        @block.tensor
        def _(pe):
            mmul = nc.tensor.matmul
            tr = nc.tensor.transpose
            pe.wait_ge(s["vconsts"], 1)
            pe.wait_ge(s["identities"], 2)
            pe.wait_ge(s["cond_act"], 1)
            tr(bank[0][:, 0:NB], cond_silu[:, 0:KA], identf[0:NB, 0:NB])
            tr(bank[0][0:KB + 1, NB:2 * NB], cond_silu[:, KA:D + 1], identf[0:NB, 0:NB]).then_inc(s["cond_T"], 1)
            pe.wait_ge(s["condT_ev"], 1)
            pe.wait_ge(s["wa_in"], 48)
            for n in range(2):
                cols = slice(n * 3 * D, (n + 1) * 3 * D)
                mmul(bank[1 + n][0:NB, 0:3 * D], condT[:, 0, :], wa_a[:, cols], start=True, stop=False)
                mmul(bank[1 + n][0:NB, 0:3 * D], condT[0:KB + 1, 1, :], wa_b[:, cols],
                     start=False, stop=True).then_inc(s["mod_mm"], 1)

            def transpose_y(dst, src):
                tr(dst[:, 0:128], src[:, 0:KA].bitcast(F32), identf[:, :])
                tr(dst[:, 128:256], src[:, Y_LO_A:YW].bitcast(F32), identf[:, :])
                return tr(dst[0:3 * KB, 256:384], src[:, KA:KA + 3 * KB].bitcast(F32), identf[:, :])

            def front_x(i, p):
                b = 2 * i + p
                pe.wait_ge(s["y_ready"], b + 1)
                if due(b):
                    pe.wait_ge(s["yT_ready"], b)
                transpose_y(bank[B_XT], y3[p]).then_inc(s["xT_done"], 1)

            def front_qkv(i, p):
                b = 2 * i + p
                pe.wait_ge(s["yT_ready"], b + 1)
                if due(2 * b - 2):
                    pe.wait_ge(s["mT_ev"], 2 * b - 2)
                dst = bank[B_QKV][:, 0:3 * D]
                mmul(dst, yT[p][:, 0, 0:128], wqkv_hi[:, :], start=True, stop=False)
                mmul(dst, yT[p][:, 0, 0:128], wqkv_lo[:, :], start=False, stop=False)
                mmul(dst, yT[p][:, 1, 0:128], wqkv_hi[:, :], start=False, stop=False)
                mmul(dst, yT[p][0:3 * KB, 2, 0:128], wqkv_rest[:, :], start=False, stop=True)\
                    .then_inc(s["qkv_done"], 1)

            def front_T(i, p, w):
                b = 2 * i + p
                if w == 0:
                    pe.wait_ge(s["stack_ready"], b + 1)
                    pe.wait_ge(s["dup_ready"], b + 1)
                    if due(b):
                        pe.wait_ge(s["kTev"], b)
                else:
                    pe.wait_ge(s["qTev"], b + 1)
                dst = bank[B_QKT][:, :].bitcast(BF16)
                for j in range(HH):
                    src = stack[p][:, (w * H + 2 * j) * HS:(w * H + 2 * j + 2) * HS]
                    last = tr(dst[:, j * 128:(j + 1) * 128], src, identb[:, :])
                last.then_inc(s[("qT_done", "kT_done")[w]], 1)

            def operand(p, w, head):
                r = 64 * (head % 2)
                return qkT[p][r:r + 64, w, head // 2, :]

            def scores_by_query(i, p, h):
                b = 2 * i + p
                if h == 0:
                    pe.wait_ge(s["kTev"], b + 1)
                if due(2 * b + h):
                    pe.wait_ge(s["max_done"], 2 * b + h)
                for n, k in enumerate(S_BANK):
                    mmul(bank[k][:, :].rearrange("p (h t) -> p h t", t=128), identb[:, :],
                         mask[:, :].unsqueeze(1).to_broadcast([128, HH // 2, 128]),
                         start=True, stop=False, skip_group_check=True)
                for n, k in enumerate(S_BANK):
                    for c in range(HH // 2):
                        head = h * HH + 2 * c + n
                        last = mmul(bank[k][:, c * 128:(c + 1) * 128], operand(p, 0, head), operand(p, 1, head),
                                    start=False, stop=True, skip_group_check=True)
                last.then_inc(s["s_done"], 1)

            def transpose_m(i, p, h, front):
                b = 2 * i + p
                if front:
                    pe.wait_ge(s["resid_ready"], b + 2)
                    pe.wait_ge(s["v_ready"], b + 2)
                pe.wait_ge(s["mm_ready"], 2 * b + h + 1)
                if due(2 * b + h):
                    pe.wait_ge(s["mT_ev"], 2 * b + h)
                tr(bank[B_QKV][:, 448:512].bitcast(BF16), mm[h][:, :], identb[:, :]).then_inc(s["mT_done"], 1)

            def scores_by_key(i, p, h):
                b = 2 * i + p
                pe.wait_ge(s["mT_ev"], 2 * b + h + 1)
                if due(2 * b + h):
                    pe.wait_ge(s["exp_done"], 2 * b + h)
                for n, k in enumerate(ST_BANK):
                    for c in range(HH // 2):
                        mmul(bank[k][:, c * 128:(c + 1) * 128], pick[:, n * HH // 2 + c, :], mT[h][:, :],
                             start=(c == 0), stop=False, skip_group_check=True)
                for n, k in enumerate(ST_BANK):
                    for c in range(HH // 2):
                        head = h * HH + 2 * c + n
                        last = mmul(bank[k][:, c * 128:(c + 1) * 128], operand(p, 1, head), operand(p, 0, head),
                                    start=False, stop=True, skip_group_check=True)
                last.then_inc(s["st_done"], 1)

            def weigh(i, p, h):
                b = 2 * i + p
                pe.wait_ge(s["p_ready"], 2 * b + h + 1)
                if h == 0:
                    if due(b):
                        pe.wait_ge(s["gated_read"], b)
                for g in range(2):
                    for q in range(4):
                        head = h * HH + 4 * g + q
                        slot = (head % 2) * (HH // 2) + (head % HH) // 2
                        last = mmul(bank[B_CTX][32 * q:32 * q + HD + 1, (2 * h + g) * 128:(2 * h + g + 1) * 128],
                                    vx[p][:, head, :], P[h][:, slot, :], start=True, stop=True)
                last.then_inc(s["pv_done"], 1)

            def context_by_token(i, p):
                b = 2 * i + p
                pe.wait_ge(s["ctxT_ev"], b + 1)
                for g in range(4):
                    last = tr(bank[B_CTX][:, g * 128:(g + 1) * 128], ctxT[:, g, :], identf[:, :])
                last.then_inc(s["tok_done"], 1)

            def context_back(i, p):
                b = 2 * i + p
                pe.wait_ge(s["ctxn_ready"], b + 1)
                tr(bank[B_CTX][:, 0:128], ctxn[:, 0:KA], identf[:, :])
                tr(bank[B_CTX][0:KB + 1, 128:256], ctxn[:, KA:D + 1], identf[:, :]).then_inc(s["back_done"], 1)

            def project(i, p):
                b = 2 * i + p
                pe.wait_ge(s["back_ev"], b + 1)
                mmul(bank[B_CTX][:, 0:D], backT[:, 0, :], wp_a[:, :], start=True, stop=False)
                mmul(bank[B_CTX][:, 0:D], backT[0:KB + 1, 1, :], wp_b[:, :], start=False, stop=True)\
                    .then_inc(s["wp_done"], 1)

            front_x(0, 0)
            front_x(0, 1)
            pe.wait_ge(s["weights"], 2)
            pe.wait_ge(s["mod_ev"], 4)
            front_qkv(0, 0)
            front_T(0, 0, 0)
            front_T(0, 0, 1)
            pe.wait_ge(s["consts"], 3)
            pe.wait_ge(s["wp_in"], 48)

            def step(i, p, tail, more):
                scores_by_query(i, p, 0)
                if tail:
                    weigh(*later(i, p, -1), 1)
                if more >= 1:
                    front_qkv(*later(i, p, 1))
                scores_by_query(i, p, 1)
                transpose_m(i, p, 0, more >= 1)
                if tail:
                    context_by_token(*later(i, p, -1))
                scores_by_key(i, p, 0)
                if more >= 2:
                    front_x(*later(i, p, 2))
                transpose_m(i, p, 1, False)
                if more >= 1:
                    front_T(*later(i, p, 1), 0)
                if tail:
                    context_back(*later(i, p, -1))
                scores_by_key(i, p, 1)
                if tail:
                    project(*later(i, p, -1))
                if more >= 1:
                    front_T(*later(i, p, 1), 1)
                weigh(i, p, 0)

            def front_x2(j):
                for t in range(2):
                    b = 2 * j + t
                    pe.wait_ge(s["y2_ready"], b + 1)
                    if due(b - 1):
                        pe.wait_ge(s["yT2_ready"], b - 1)
                    transpose_y(bank[t], y3[t]).then_inc(s["xT2_done"], 1)

            def expand(j, q, chunks):
                pe.wait_ge(s["yT2_ready"], 2 * j + 2)
                for c in chunks:
                    n = 128 if c < FC - 1 else FL
                    f = slice(c * 128, c * 128 + n)
                    dst = bank[H_BANK[c]][0:n, 0:256]
                    before = FC * j + c - 2 if c >= 3 else FC * (j - 1) + (FC - 1, FC, 3)[c]
                    if due(before):
                        pe.wait_ge(s["silu_done"], before)
                    mmul(dst, w1_hi[:, f], yT[q][:, 0, :], start=True, stop=False)
                    mmul(dst, w1_hi[:, f], yT[q][:, 1, :], start=False, stop=False)
                    mmul(dst, w1_lo[:, f], yT[q][:, 0, :], start=False, stop=False)
                    mmul(dst, w1_rest[:, f], yT[q][0:3 * KB, 2, :], start=False, stop=True)\
                        .then_inc(s["w1_done"], 1)

            def contract(j, q):
                for t in range(2):
                    b = 2 * j + t
                    if due(b - 1):
                        pe.wait_ge(s["gated2_ready"], b - 1)
                    for c in range(FC):
                        n = 128 if c < FC - 1 else FL + 1
                        if t == 0:
                            pe.wait_ge(s["silu_done"], FC * j + c + 1)
                        last = mmul(bank[5 + t][:, 0:D], hT[q][0:n, c, t * 128:(t + 1) * 128], w2[0:n, c, :],
                                    start=(c == 0), stop=(c == FC - 1))
                    last.then_inc(s["w2_done"], 1)

            def pair(j, q, front):
                expand(j, q, range(FC))
                if front:
                    front_x2(j + 1)
                contract(j, q)

            sequences(pe, step)
            last = (NPAIR - 1, 1)
            pe.wait_ge(s["weights"], 4)
            pe.wait_ge(s["w2_in"], 48)
            pe.wait_ge(s["mT_ev"], 2 * NB)
            front_x2(0)
            weigh(*last, 1)
            expand(0, 0, (0,))
            context_by_token(*last)
            expand(0, 0, (1,))
            context_back(*last)
            expand(0, 0, (2,))
            project(*last)
            expand(0, 0, (3, 4))
            front_x2(1)
            contract(0, 0)
            with pe.Fori(0, (NPAIR - 2) // 2) as k:
                pair(2 * k + 1, 1, True)
                pair(2 * k + 2, 0, True)
            pair(NPAIR - 1, 1, False)


_INS = ['x', 'cond_1152', 'L0_cond_Wq', 'L0_cond_Wk', 'L0_cond_Wv', 'L0_cond_Wp', 'L0_cond_bp', 'L0_cond_W1',
        'L0_cond_b1', 'L0_cond_W2', 'L0_cond_b2', 'L0_cond_Wa', 'L0_cond_ba']


def kernel(**inputs):
    import numpy as _np
    import concourse.bacc as _bacc
    from concourse import mybir as _mybir
    from concourse.bass_utils import run_bass_kernel_spmd as _run

    nc = _bacc.Bacc("TRN2", target_bir_lowering=False, num_devices=1)
    arrays, args = {}, []
    for name in _INS:
        a = _np.ascontiguousarray(inputs[name])
        arrays[f"in_{name}"] = a
        args.append(nc.dram_tensor(f"in_{name}", a.shape, _mybir.dt.from_np(a.dtype), kind="ExternalInput").ap())
    out = nc.dram_tensor("out", (NB, T, D), F32, kind="ExternalOutput").ap()
    build(nc, *args, out)
    r = _run(nc, [arrays], core_ids=[0])
    return r.results[0]["out"]
```

```python
from contextlib import ExitStack

import numpy as np

import concourse.bass as bass
from concourse import mybir

F32 = mybir.dt.float32
F32R = mybir.dt.float32r
BF16 = mybir.dt.bfloat16
ALU = mybir.AluOpType
ACT = mybir.ActivationFunctionType
AX = mybir.AxisListType

NB, T, D = 32, 128, 144
H = 16
HD = D // H
FF = 4 * D
EPS = 1e-6
SCALE = float(1.0 / np.sqrt(HD))
KA = 128
KB = D - KA
HH = H // 2
FC = (FF + 127) // 128
FL = FF - (FC - 1) * 128
MASKED = -3.0e38
Y_LO_B, Y_HI_B, Y_LO_A = D, D + KB, D + 2 * KB
YW = D + 2 * KB + KA
HS = 64
M_ROW = 6 * HD


def slots(q, k):
    return q * HD, H * HS + (k - q) * HD


def build(nc, x, cond, Wq, Wk, Wv, Wp, bp, W1, b1, W2, b2, Wa, ba, out):
    mod_dram = nc.dram_tensor("modulation", [NB, 6 * D], F32, kind="Internal").ap()
    ctx = ExitStack()
    with ctx:
        def sb(name, shape, dt=F32):
            return ctx.enter_context(nc.sbuf_tensor(name, shape, dt))

        def sem(name):
            return ctx.enter_context(nc.semaphore(name))

        def view(t, offset, dims, parts=128):
            width = int(np.prod(t.shape[1:]))
            return bass.AP(t, offset, [[width, parts], *dims])

        def slot_pair(p, q, k):
            offset, step = slots(q, k)
            return view(stack[p], offset, [[step, 2], [HS, H], [1, HD]])

        identf = sb("identf", [128, 128])
        identb = sb("identb", [128, 128], BF16)
        mask = sb("mask", [128, 128], BF16)
        wqkv = sb("wqkv", [128, 3 * D])
        wqkv_tail = sb("wqkv_tail", [3 * KB, 3 * D])
        w1 = sb("w1", [128, FF])
        w1_tail = sb("w1_tail", [3 * KB, FF])
        wqkv_hi = sb("wqkv_hi", [128, 3 * D], F32R)
        wqkv_lo = sb("wqkv_lo", [128, 3 * D], F32R)
        wqkv_rest = sb("wqkv_rest", [3 * KB, 3 * D], F32R)
        w1_hi = sb("w1_hi", [128, FF], F32R)
        w1_lo = sb("w1_lo", [128, FF], F32R)
        w1_rest = sb("w1_rest", [3 * KB, FF], F32R)
        wp_a = sb("wp_a", [128, D])
        wp_b = sb("wp_b", [KB + 1, D])
        w2 = sb("w2", [128, FC, D])
        b1c = sb("b1c", [128, FC])
        wa_a = sb("wa_a", [128, 6 * D])
        wa_b = sb("wa_b", [KB + 1, 6 * D])
        cond_sb = sb("cond_sb", [NB, D])
        cond_silu = sb("cond_silu", [NB, D + 1])
        condT = sb("condT", [128, 2, NB])
        mod = sb("mod", [NB, 6 * D])
        xr = sb("xr", [128, NB, D])
        st1 = sb("st1", [128, NB, 6])
        st2 = sb("st2", [128, NB, 6])
        mean_gap = sb("mean_gap", [128, NB])
        mean_sum = sb("mean_sum", [128, NB])
        within = sb("within", [128, NB])
        across = sb("across", [128, NB])
        ve = sb("ve", [128, NB])
        sd = sb("sd", [128, NB])
        rsd = sb("rsd", [128, NB])
        rstd = sb("rstd", [128, NB])
        nmr = sb("nmr", [128, NB])
        bcm = [sb(f"bcm{p}", [128, 2 * D]) for p in range(2)]
        bcg = [sb(f"bcg{p}", [128, D]) for p in range(2)]
        tn = [sb(f"tn{p}", [128, D]) for p in range(2)]
        ts = [sb(f"ts{p}", [128, D]) for p in range(2)]
        ym = [sb(f"ym{p}", [128, D]) for p in range(2)]
        y3 = [sb(f"y3{p}", [128, YW], F32R) for p in range(2)]
        yT = [sb(f"yT{p}", [128, 3, 256], F32R) for p in range(2)]
        stack = [sb(f"stack{p}", [128, 2 * H * HS], BF16) for p in range(2)]
        resid = [sb(f"resid{p}", [128, 2 * D]) for p in range(2)]
        vx = [sb(f"vx{u}", [128, H, HD + 1]) for u in range(4)]
        qkT = [sb(f"qkT{u}", [128, 2, HH, 128], BF16) for u in range(4)]
        mx = sb("mx", [128, 2, HH])
        mm = [sb(f"mm{h}", [128, 2, 2, HH // 2], BF16) for h in range(2)]
        mT = [sb(f"mT{h}", [2 * HH, 128], BF16) for h in range(2)]
        P = [sb(f"P{h}", [128, HH, 128]) for h in range(2)]
        ctxT = sb("ctxT", [128, 4, 128])
        rden = sb("rden", [128, H])
        ctxn = sb("ctxn", [128, D + 1])
        backT = sb("backT", [128, 2, 128])
        gated = sb("gated", [128, D])
        hT = [sb(f"hT{p}", [128, FC, 256]) for p in range(2)]
        gated2 = [sb(f"gated2{t}", [128, D]) for t in range(2)]

        bank = [ctx.enter_context(nc.psum_tensor(f"bank{i}", [128, 512], F32)) for i in range(8)]
        B_XT, B_QKV, B_QKT, B_CTX = 0, 1, 2, 7
        S_BANK = (3, 4)
        ST_BANK = (5, 6)
        H_BANK = (2, 3, 4, 2, 3)

        m_slot = (bank[B_XT][0:2 * HH, 384:448].bitcast(BF16), bank[B_QKV][0:2 * HH, 448:512].bitcast(BF16))

        s = {n: sem(n) for n in (
            "x_in0 x_in1 x_in2 x_in3 cond_in wa_in wqkv_in w1_in wp_in w2_in b1_in "
            "mod_out0 mod_out1 bcm_in0 bcm_in1 bcg_in0 bcg_in1 out_done "
            "identities consts vconsts cond_act cond_T condT_ev mod_mm mod_ev weights w1_high w1_split "
            "stats moments ve_ready sd_ready nchain norm_ready "
            "t_ready scaled ym_ready yhi_ready y_ready xT_done yT_ready qkv_done qk_high v_ready resid_ready "
            "mid_ready stack_ready dup_ready qT_done kT_done qTev kTev "
            "s_done max_done mhi mm_ready mT_done mT_ev m_placed0 m_placed1 st_done exp_done p_ready pv_done "
            "ctxT_ev tok_done rden_ready ctxn_ready back_done back_ev wp_done gated_read x1_ready stats2 "
            "bc2_in0 bc2_in1 t2_ready scaled2 ym2_ready yhi2_ready y2_ready xT2_done yT2_ready w1_done silu_done w2_done "
            "gated2_ready result_ready").split()}

        def due(count):
            return not (isinstance(count, int) and count <= 0)

        def later(i, u, d):
            return i + (u + d) // 4, (u + d) % 4

        def sequences(eng, step):
            for b in range(4):
                step(0, b, min(b, 2), 3)
            with eng.Fori(1, NB // 4 - 1) as i:
                for u in range(4):
                    step(i, u, 2, 3)
            for b in range(NB - 4, NB + 1):
                step(b // 4, b % 4, 2, NB - 1 - b)

        LAST = (NB // 4 - 1, 3)
        XG = NB // 4
        NEARLY = NB - 4
        NPAIR = NB // 2
        block = ctx.enter_context(nc.Block())

        @block.sync
        def _(sp):
            xv = x.rearrange("b t d -> t b d")

            def load_x(g):
                sp.dma_start(xr[:, g * XG:(g + 1) * XG, :], xv[:, g * XG:(g + 1) * XG, :])\
                    .then_inc(s[f"x_in{g}"], 16)

            sp.dma_start(cond_sb[:, :], cond).then_inc(s["cond_in"], 16)
            sp.dma_start(wa_a[:, :], Wa[0:KA, :]).then_inc(s["wa_in"], 16)
            sp.dma_start(wa_b[0:KB, :], Wa[KA:D, :]).then_inc(s["wa_in"], 16)
            sp.dma_start(wa_b[KB:KB + 1, :], ba.unsqueeze(0)).then_inc(s["wa_in"], 16)
            load_x(0)

            def thrice(w, width):
                return w[KA:D, :].unsqueeze(0).to_broadcast([3, KB, width])

            for n, w in enumerate((Wq, Wk, Wv)):
                sp.dma_start(wqkv[:, n * D:(n + 1) * D], w[0:KA, :]).then_inc(s["wqkv_in"], 16)
                sp.dma_start(wqkv_tail[:, n * D:(n + 1) * D], thrice(w, D)).then_inc(s["wqkv_in"], 16)
            load_x(1)
            sp.wait_ge(s["mod_ev"], 2)
            sp.dma_start(mod_dram[:, 0:3 * D], mod[:, 0:3 * D]).then_inc(s["mod_out0"], 16)
            sp.dma_start(wp_a[:, :], Wp[0:KA, :]).then_inc(s["wp_in"], 16)
            sp.dma_start(wp_b[0:KB, :], Wp[KA:D, :]).then_inc(s["wp_in"], 16)
            sp.dma_start(wp_b[KB:KB + 1, :], bp.unsqueeze(0)).then_inc(s["wp_in"], 16)
            sp.wait_ge(s["mod_out0"], 16)

            def row(b, lo, n):
                return mod_dram[bass.ds(b, 1), lo:lo + n].to_broadcast([128, n]) if not isinstance(b, int) \
                    else mod_dram[b:b + 1, lo:lo + n].to_broadcast([128, n])

            def load_modulation(i, u):
                b, p = 4 * i + u, u % 2
                if due(b - 1):
                    sp.wait_ge(s["ym_ready"], b - 1)
                sp.dma_start(bcm[p][:, :], row(b, 0, 2 * D)).then_inc(s[f"bcm_in{p}"], 16)

            def load_gate(i, u):
                b, p = 4 * i + u, u % 2
                if due(b - 1):
                    sp.wait_ge(s["gated_read"], b - 1)
                sp.dma_start(bcg[p][:, :], row(b, 2 * D, D)).then_inc(s[f"bcg_in{p}"], 16)

            def place_maxima(i, u, h):
                b = 4 * i + u
                sp.wait_ge(s["mT_ev"], 2 * b + h + 1)
                for n in range(2):
                    r = 64 * n + M_ROW
                    sp.dma_start(qkT[u][r:r + 2, 0, h * HH // 2:(h + 1) * HH // 2, :],
                                 mT[h][n * HH:(n + 1) * HH, :]).then_inc(s[f"m_placed{h}"], 16)

            def load2(j, t):
                b = 2 * j + t
                if due(b - 1):
                    sp.wait_ge(s["ym2_ready"], b - 1)
                sp.dma_start(bcm[t][:, :], row(b, 3 * D, 2 * D)).then_inc(s[f"bc2_in{t}"], 16)

            def gate2(j, t):
                b = 2 * j + t
                if isinstance(j, int) and j == 0:
                    sp.wait_ge(s["gated_read"], NB)
                if due(b - 1):
                    sp.wait_ge(s["gated2_ready"], b - 1)
                sp.dma_start(bcg[t][:, :], row(b, 5 * D, D)).then_inc(s[f"bcg_in{t}"], 16)

            def step(i, u, behind, more):
                if more >= 3:
                    load_modulation(*later(i, u, 3))
                if more == 1:
                    sp.wait_ge(s["mod_out1"], 16)
                    sp.wait_ge(s["ym_ready"], NB)
                    load2(0, 0)
                    load2(0, 1)
                if behind >= 1:
                    load_gate(*later(i, u, -1))
                if more >= 0:
                    place_maxima(i, u, 0)
                    place_maxima(i, u, 1)
                else:
                    load2(1, 0)
                    load2(1, 1)

            load_modulation(0, 0)
            load_modulation(0, 1)
            load_x(2)
            load_x(3)
            sp.dma_start(w1[:, :], W1[0:KA, :]).then_inc(s["w1_in"], 16)
            sp.dma_start(w1_tail[:, :], thrice(W1, FF)).then_inc(s["w1_in"], 16)
            sp.dma_start(w2[:, 0:FC - 1, :], W2[0:(FC - 1) * 128, :].rearrange("(c p) d -> p c d", p=128))\
                .then_inc(s["w2_in"], 16)
            sp.dma_start(w2[0:FL, FC - 1, :], W2[(FC - 1) * 128:FF, :]).then_inc(s["w2_in"], 16)
            sp.dma_start(w2[FL:FL + 1, FC - 1, :], b2.unsqueeze(0)).then_inc(s["w2_in"], 16)
            with nc.allow_non_contiguous_dma(reason="the bias of the hidden layer, one element a partition"):
                sp.dma_start(b1c[:, 0:FC - 1], b1[0:(FC - 1) * 128].rearrange("(c p) -> p c", p=128))\
                    .then_inc(s["b1_in"], 16)
                sp.dma_start(b1c[0:FL, FC - 1:FC], b1[(FC - 1) * 128:FF].unsqueeze(1)).then_inc(s["b1_in"], 16)
            load_modulation(0, 2)
            sp.wait_ge(s["mod_ev"], 4)
            sp.dma_start(mod_dram[:, 3 * D:6 * D], mod[:, 3 * D:6 * D]).then_inc(s["mod_out1"], 16)
            sequences(sp, step)

            def pair2(j, stored, ahead):
                if ahead:
                    load2(j + 2, 0)
                gate2(j, 0)
                gate2(j, 1)
                if stored:
                    store(j - 1)
                if ahead:
                    load2(j + 2, 1)

            def store(j):
                sp.wait_ge(s["result_ready"], 2 * j + 2)
                sp.dma_start(out.rearrange("b t d -> t b d")[:, bass.ds(2 * j, 2), :],
                             xr[:, bass.ds(2 * j, 2), :]).then_inc(s["out_done"], 16)

            pair2(0, False, True)
            with sp.Fori(1, NPAIR - 2) as j:
                pair2(j, True, True)
            pair2(NPAIR - 2, True, False)
            pair2(NPAIR - 1, True, False)
            store(NPAIR - 1)
            sp.wait_ge(s["out_done"], 16 * NPAIR)

        @block.gpsimd
        def _(pool):
            g = nc.gpsimd
            g.memset(identf[:, :], 0.0)
            g.memset(identb[:, :], 0.0).then_inc(s["identities"], 1)
            pool.wait_ge(s["identities"], 1)
            for m in (identf, identb):
                last = g.affine_select(out=m[:, :], in_=m[:, :], compare_op=ALU.not_equal, fill=1.0, base=0,
                                       pattern=[[-1, 128]], channel_multiplier=1)
            last.then_inc(s["identities"], 1)
            g.memset(mask[:, :], 0.0)
            g.memset(ctxn[:, D:D + 1], 1.0)
            for u in range(4):
                last = g.memset(vx[u][:, :, :], 1.0)
            last.then_inc(s["consts"], 1)
            pool.wait_ge(s["consts"], 1)
            g.affine_select(out=mask[:, :], in_=mask[:, :], compare_op=ALU.is_ge, fill=MASKED, base=0,
                            pattern=[[-1, 128]], channel_multiplier=1).then_inc(s["consts"], 1)

            def standing():
                pool.nop(nofuse=True)

            def modulate(b, p, ready, arrived, count, scaled, ym_ready, yhi, y_ready, used, used_count):
                pool.wait_ge(s[arrived], count)
                pool.wait_ge(s[ready], b + 1)
                g.tensor_tensor(ts[p][:, :], tn[p][:, :], bcm[p][:, D:2 * D], ALU.mult).then_inc(s[scaled], 1)
                pool.wait_ge(s[scaled], b + 1)
                g.tensor_tensor(ym[p][:, :], ts[p][:, :], bcm[p][:, 0:D], ALU.add).then_inc(s[ym_ready], 1)
                pool.wait_ge(s[ym_ready], b + 1)
                if due(used_count):
                    pool.wait_ge(s[used], used_count)
                standing()
                g.tensor_scalar(y3[p][:, 0:D], ym[p][:, :], 1.0, 0.0, ALU.mult, ALU.add).then_inc(s[yhi], 1)
                g.tensor_scalar(y3[p][:, Y_HI_B:Y_HI_B + KB], ym[p][:, KA:D], 1.0, 0.0, ALU.mult, ALU.add)
                pool.wait_ge(s[yhi], b + 1)
                g.tensor_tensor(y3[p][:, Y_LO_B:Y_LO_B + KB], ym[p][:, KA:D], y3[p][:, KA:D].bitcast(F32),
                                ALU.subtract)
                g.tensor_tensor(y3[p][:, Y_LO_A:YW], ym[p][:, 0:KA], y3[p][:, 0:KA].bitcast(F32), ALU.subtract)\
                    .then_inc(s[y_ready], 1)

            def modulate1(i, u):
                b, p = 4 * i + u, u % 2
                modulate(b, p, "t_ready", f"bcm_in{p}", 16 * (2 * i + u // 2) + 16, "scaled", "ym_ready", "yhi_ready", "y_ready",
                         "xT_done", b - 1)

            def split(i, u):
                b, p = 4 * i + u, u % 2
                pool.wait_ge(s["resid_ready"], b + 1)
                standing()
                r = view(resid[p], 0, [[D, 2], [HD, H], [1, HD]])
                mid = slot_pair(p, 2, 2)
                g.tensor_scalar(mid, r, 1.0, 0.0, ALU.mult, ALU.add).then_inc(s["mid_ready"], 1)
                g.tensor_scalar(slot_pair(p, 3, 1), r, 1.0, 0.0, ALU.mult, ALU.add)
                pool.wait_ge(s["mid_ready"], b + 1)
                g.tensor_tensor(slot_pair(p, 5, 4), r, mid, ALU.subtract).then_inc(s["stack_ready"], 1)

            def select(i, u, h):
                b = 4 * i + u
                pool.wait_ge(s["exp_done"], 4 * b + 2 * h + 2)
                standing()
                g.affine_select(out=P[h][:, :, :], in_=P[h][:, :, :], compare_op=ALU.is_ge, fill=0.0,
                                base=0, pattern=[[0, HH], [1, 128]], channel_multiplier=-1)\
                    .then_inc(s["p_ready"], 1)

            def split_w1():
                pool.wait_ge(s["w1_in"], 2 * 16)
                g.tensor_scalar(w1_hi[:, :], w1[:, :], 1.0, 0.0, ALU.mult, ALU.add)
                g.tensor_scalar(w1_rest[:, :], w1_tail[:, :], 1.0, 0.0, ALU.mult, ALU.add)\
                    .then_inc(s["w1_high"], 1)
                pool.wait_ge(s["w1_high"], 1)
                g.tensor_tensor(w1_lo[:, :], w1[:, :], w1_hi[:, :].bitcast(F32), ALU.subtract)\
                    .then_inc(s["w1_high"], 1)
                pool.wait_ge(s["w1_high"], 2)
                g.tensor_tensor(w1_rest[2 * KB:3 * KB, :], w1_tail[2 * KB:3 * KB, :],
                                w1_rest[2 * KB:3 * KB, :].bitcast(F32), ALU.subtract)\
                    .then_inc(s["w1_split"], 1)
                pool.wait_ge(s["w1_split"], 1)

            modulate1(0, 0)
            modulate1(0, 1)
            split(0, 0)
            modulate1(0, 2)

            def step(i, u, behind, more):
                if more >= 1:
                    split(*later(i, u, 1))
                if behind == 0:
                    split_w1()
                for h in range(2):
                    if behind >= 1:
                        select(*later(i, u, -1), h)
                    if more == 0:
                        modulate2(0, h)
                if more >= 3:
                    modulate1(*later(i, u, 3))
                if more < 0:
                    modulate2(1, 0)
                    modulate2(1, 1)

            def modulate2(j, t):
                b = 2 * j + t
                modulate(b, t, "t2_ready", f"bc2_in{t}", 16 * j + 16, "scaled2", "ym2_ready", "yhi2_ready",
                         "y2_ready", "xT2_done", b - 1)

            sequences(pool, step)
            with pool.Fori(2, NPAIR) as j:
                modulate2(j, 0)
                modulate2(j, 1)

        @block.scalar
        def _(act):
            a = nc.scalar

            def deviation(times, lo, hi):
                act.wait_ge(s["ve_ready"], times)
                a.activation(sd[:, lo:hi], ve[:, lo:hi], ACT.Sqrt).then_inc(s["sd_ready"], 1)

            act.wait_ge(s["vconsts"], 1)
            act.wait_ge(s["cond_in"], 16)
            a.activation(cond_silu[:, 0:D], cond_sb[:, :], ACT.Silu).then_inc(s["cond_act"], 1)
            act.wait_ge(s["cond_T"], 1)
            a.copy(condT[:, 0, :], bank[0][:, 0:NB])
            a.copy(condT[0:KB + 1, 1, :], bank[0][0:KB + 1, NB:2 * NB]).then_inc(s["condT_ev"], 1)
            deviation(1, 0, XG)
            for n in range(2):
                dst = mod[:, n * 3 * D:(n + 1) * 3 * D].rearrange("p (n d) -> p n d", n=3)
                src = bank[1 + n][0:NB, 0:3 * D].rearrange("p (n d) -> p n d", n=3)
                act.wait_ge(s["mod_mm"], n + 1)
                a.copy(dst[:, 0:3:2, :], src[:, 0:3:2, :]).then_inc(s["mod_ev"], 1)
                a.add(dst[:, 1, :], src[:, 1, :], 1.0).then_inc(s["mod_ev"], 1)

            def evacuate_y(i, u):
                b, p = 4 * i + u, u % 2
                act.wait_ge(s["xT_done"], b + 1)
                a.copy(yT[p][:, 0:2, 0:128], bank[B_XT][:, 0:256].rearrange("p (c t) -> p c t", c=2))
                a.copy(yT[p][0:3 * KB, 2, 0:128], bank[B_XT][0:3 * KB, 256:384]).then_inc(s["yT_ready"], 1)

            def evacuate_qkv(i, u):
                b, p = 4 * i + u, u % 2
                act.wait_ge(s["qkv_done"], b + 1)
                if due(b - 1):
                    act.wait_ge(s["kT_done"], b - 1)
                a.copy(slot_pair(p, 0, 0),
                       bank[B_QKV][:, 0:2 * D].rearrange("p (w h d) -> p w h d", w=2, h=H))\
                    .then_inc(s["qk_high"], 1)
                if due(2 * b - 6):
                    act.wait_ge(s["pv_done"], 2 * b - 6)
                a.copy(vx[u][:, :, 0:HD], bank[B_QKV][:, 2 * D:3 * D].rearrange("p (h d) -> p h d", h=H))\
                    .then_inc(s["v_ready"], 1)

            def evacuate_mT(i, u, h):
                b = 4 * i + u
                act.wait_ge(s["mT_done"], 2 * b + h + 1)
                if due(32 * b):
                    act.wait_ge(s[f"m_placed{h}"], 32 * b)
                a.copy(mT[h][:, :], m_slot[h]).then_inc(s["mT_ev"], 1)

            def exponentials(i, u, h, n):
                b = 4 * i + u
                act.wait_ge(s["st_done"], 4 * b + 2 * h + n + 1)
                if n == 0:
                    if due(2 * b + h - 1):
                        act.wait_ge(s["pv_done"], 2 * b + h - 1)
                a.activation(P[h][:, n * HH // 2:(n + 1) * HH // 2, :],
                             bank[ST_BANK[n]][:, :].rearrange("p (h t) -> p h t", t=128), ACT.Exp,
                             scale=SCALE).then_inc(s["exp_done"], 1)

            def evacuate_ctx(i, u):
                b = 4 * i + u
                act.wait_ge(s["pv_done"], 2 * b + 2)
                if due(b):
                    act.wait_ge(s["tok_done"], b)
                a.copy(ctxT[:, :, :], bank[B_CTX][:, :].rearrange("p (g t) -> p g t", t=128))\
                    .then_inc(s["ctxT_ev"], 1)

            def evacuate_back(i, u):
                b = 4 * i + u
                act.wait_ge(s["back_done"], b + 1)
                if due(b):
                    act.wait_ge(s["wp_done"], b)
                a.copy(backT[:, 0, :], bank[B_CTX][:, 0:128])
                a.copy(backT[0:KB + 1, 1, :], bank[B_CTX][0:KB + 1, 128:256]).then_inc(s["back_ev"], 1)

            evacuate_y(0, 0)
            evacuate_qkv(0, 0)
            evacuate_y(0, 1)
            deviation(2, XG, NB)

            def step(i, u, behind, more):
                if more == 1:
                    deviation(3, 0, NEARLY)
                if more >= 1:
                    evacuate_qkv(*later(i, u, 1))
                if behind >= 2:
                    evacuate_ctx(*later(i, u, -2))
                if behind >= 1:
                    exponentials(*later(i, u, -1), 0, 0)
                    exponentials(*later(i, u, -1), 0, 1)
                if behind >= 2:
                    evacuate_back(*later(i, u, -2))
                if more >= 0:
                    evacuate_mT(i, u, 0)
                if behind >= 1:
                    exponentials(*later(i, u, -1), 1, 0)
                    exponentials(*later(i, u, -1), 1, 1)
                if more >= 2:
                    evacuate_y(*later(i, u, 2))
                if more >= 0:
                    evacuate_mT(i, u, 1)

            sequences(act, step)

            def hidden(j, q, chunks):
                for c in chunks:
                    n = 128 if c < FC - 1 else FL
                    act.wait_ge(s["w1_done"], FC * j + c + 1)
                    if c == 0:
                        if due(2 * j - 2):
                            act.wait_ge(s["w2_done"], 2 * j - 2)
                    a.activation(hT[q][0:n, c, :], bank[H_BANK[c]][0:n, 0:256], ACT.Silu,
                                 bias=b1c[0:n, c:c + 1]).then_inc(s["silu_done"], 1)

            act.wait_ge(s["b1_in"], 32)
            evacuate_ctx(*LAST)
            hidden(0, 0, (0,))
            evacuate_back(*LAST)
            hidden(0, 0, range(1, FC))
            deviation(4, NEARLY, NB)
            hidden(1, 1, range(FC))
            with act.Fori(1, NPAIR // 2) as k:
                hidden(2 * k, 0, range(FC))
                hidden(2 * k + 1, 1, range(FC))

        @block.vector
        def _(dve):
            v = nc.vector
            v.memset(cond_silu[:, D:D + 1], 1.0)
            for q in range(2):
                v.memset(hT[q][FL:FL + 1, FC - 1, :], 1.0)
            for p in range(2):
                v.memset(view(stack[p], M_ROW, [[HS, H], [1, HS - M_ROW]]), 0.0)
                v.memset(view(stack[p], H * HS + M_ROW, [[HS, H], [1, HS - M_ROW]]), -1.0)
            v.memset(bank[B_CTX][:, :], 0.0).then_inc(s["vconsts"], 1)

            def first_statistics(n):
                dve.wait_ge(s[f"x_in{n}"], 16)
                for b in range(n * XG, (n + 1) * XG):
                    last = v.bn_stats(st1[:, b, :], xr[:, b, :])
                last.then_inc(s["stats"], 1)

            def moments(times, st, lo, hi):
                g = slice(lo, hi)
                v.tensor_tensor(mean_gap[:, g], st[:, g, 1], st[:, g, 4], ALU.subtract)
                v.tensor_tensor(mean_sum[:, g], st[:, g, 1], st[:, g, 4], ALU.add)
                v.tensor_tensor(within[:, g], st[:, g, 2], st[:, g, 5], ALU.add).then_inc(s["moments"], 1)
                dve.wait_ge(s["moments"], 2 * times - 1)
                v.scalar_tensor_tensor(out=across[:, g], in0=mean_gap[:, g], scalar=0.25, in1=mean_gap[:, g],
                                       op0=ALU.mult, op1=ALU.mult)
                v.tensor_scalar(within[:, g], within[:, g], 1.0 / D, EPS, ALU.mult, ALU.add)\
                    .then_inc(s["moments"], 1)
                dve.wait_ge(s["moments"], 2 * times)
                v.tensor_tensor(ve[:, g], within[:, g], across[:, g], ALU.add).then_inc(s["ve_ready"], 1)

            def inverse_deviation(times, lo, hi):
                g = slice(lo, hi)
                base = 4 * (times - 1)
                dve.wait_ge(s["sd_ready"], times)
                v.reciprocal(rsd[:, g], sd[:, g]).then_inc(s["nchain"], 1)
                dve.wait_ge(s["nchain"], base + 1)
                v.tensor_tensor(rsd[:, g], rsd[:, g], ve[:, g], ALU.mult).then_inc(s["nchain"], 1)
                dve.wait_ge(s["nchain"], base + 2)
                v.tensor_tensor(rsd[:, g], rsd[:, g], sd[:, g], ALU.add).then_inc(s["nchain"], 1)
                dve.wait_ge(s["nchain"], base + 3)
                v.reciprocal(rstd[:, g], rsd[:, g]).then_inc(s["nchain"], 1)
                dve.wait_ge(s["nchain"], base + 4)
                v.tensor_scalar(rstd[:, g], rstd[:, g], 2.0, None, ALU.mult).then_inc(s["norm_ready"], 1)
                dve.wait_ge(s["norm_ready"], 2 * times - 1)
                v.scalar_tensor_tensor(out=nmr[:, g], in0=mean_sum[:, g], scalar=-0.5, in1=rstd[:, g],
                                       op0=ALU.mult, op1=ALU.mult).then_inc(s["norm_ready"], 1)
                dve.wait_ge(s["norm_ready"], 2 * times)

            def normalize(b, p, name, used):
                if due(b - 1):
                    dve.wait_ge(s[used], b - 1)
                v.tensor_scalar(tn[p][:, :], xr[:, b, :] if isinstance(b, int) else xr[:, bass.ds(b, 1), :],
                                rstd[:, bass.ds(b, 1)], nmr[:, bass.ds(b, 1)], ALU.mult, ALU.add)\
                    .then_inc(s[name], 1)

            def residuals(i, u):
                b, p = 4 * i + u, u % 2
                dve.wait_ge(s["v_ready"], b + 1)
                if due(b - 1):
                    dve.wait_ge(s["stack_ready"], b - 1)
                hi = slot_pair(p, 0, 0)
                v.tensor_tensor(resid[p][:, :].rearrange("p (w h d) -> p w h d", w=2, h=H),
                                bank[B_QKV][:, 0:2 * D].rearrange("p (w h d) -> p w h d", w=2, h=H),
                                hi, ALU.subtract).then_inc(s["resid_ready"], 1)

            def copies(i, u):
                b, p = 4 * i + u, u % 2
                dve.wait_ge(s["qk_high"], b + 1)
                hi = slot_pair(p, 0, 0)
                v.tensor_copy(slot_pair(p, 1, 3), hi)
                v.tensor_copy(slot_pair(p, 4, 5), hi).then_inc(s["dup_ready"], 1)

            def maxima(i, u, h):
                b = 4 * i + u
                for n, k in enumerate(S_BANK):
                    dve.wait_ge(s["s_done"], 4 * b + 2 * h + n + 1)
                    v.tensor_reduce(mx[:, h, n * HH // 2:(n + 1) * HH // 2],
                                    bank[k][:, :].rearrange("p (h t) -> p h t", t=128), AX.X, ALU.max)\
                        .then_inc(s["max_done"], 1)

            def maxima_high(i, u, h):
                b = 4 * i + u
                dve.wait_ge(s["max_done"], 4 * b + 2 * h + 2)
                if due(2 * b + h - 1):
                    dve.wait_ge(s["mT_done"], 2 * b + h - 1)
                v.tensor_copy(mm[h][:, :, 0, :], mx[:, h, :].rearrange("p (n c) -> p n c", n=2))\
                    .then_inc(s["mhi"], 1)

            def maxima_low(i, u, h):
                b = 4 * i + u
                dve.wait_ge(s["mhi"], 2 * b + h + 1)
                v.tensor_tensor(mm[h][:, :, 1, :], mx[:, h, :].rearrange("p (n c) -> p n c", n=2),
                                mm[h][:, :, 0, :], ALU.subtract).then_inc(s["mm_ready"], 1)

            def evacuate_T(i, u, w):
                b = 4 * i + u
                dve.wait_ge(s[("qT_done", "kT_done")[w]], b + 1)
                if due(4 * b - 12):
                    dve.wait_ge(s["st_done"], 4 * b - 12)
                v.tensor_copy(qkT[u][:, w, :, :], bank[B_QKT][:, :].bitcast(BF16)
                              .rearrange("p (j t) -> p j t", t=128)).then_inc(s[("qTev", "kTev")[w]], 1)

            def invert_sums(i, u):
                b = 4 * i + u
                tok = bank[B_CTX][:, :].rearrange("p (h c) -> p h c", c=32)
                dve.wait_ge(s["tok_done"], b + 1)
                v.reciprocal(rden[:, :], tok[:, :, HD]).then_inc(s["rden_ready"], 1)

            def divide(i, u):
                b = 4 * i + u
                tok = bank[B_CTX][:, :].rearrange("p (h c) -> p h c", c=32)
                dve.wait_ge(s["rden_ready"], b + 1)
                if due(b):
                    dve.wait_ge(s["back_done"], b)
                v.tensor_tensor(ctxn[:, 0:D].rearrange("p (h d) -> p h d", d=HD), tok[:, :, 0:HD],
                                rden[:, :].unsqueeze(2).to_broadcast([128, H, HD]), ALU.mult)\
                    .then_inc(s["ctxn_ready"], 1)

            def gate_attention(i, u):
                b, p = 4 * i + u, u % 2
                dve.wait_ge(s["wp_done"], b + 1)
                dve.wait_ge(s[f"bcg_in{p}"], 16 * (2 * i + u // 2) + 16)
                v.tensor_tensor(gated[:, :], bank[B_CTX][:, 0:D], bcg[p][:, :], ALU.mult)\
                    .then_inc(s["gated_read"], 1)

            def add_attention(i, u):
                b = 4 * i + u
                dve.wait_ge(s["gated_read"], b + 1)
                row = xr[:, bass.ds(b, 1), :]
                v.tensor_tensor(row, row, gated[:, :].unsqueeze(1), ALU.add).then_inc(s["x1_ready"], 1)

            def statistics(i, u):
                b = 4 * i + u
                dve.wait_ge(s["x1_ready"], b + 1)
                v.bn_stats(st2[:, bass.ds(b, 1), :], xr[:, bass.ds(b, 1), :]).then_inc(s["stats2"], 1)

            first_statistics(0)
            dve.wait_ge(s["stats"], 1)
            moments(1, st1, 0, XG)
            inverse_deviation(1, 0, XG)
            normalize(0, 0, "t_ready", "scaled")
            normalize(1, 1, "t_ready", "scaled")
            dve.wait_ge(s["wqkv_in"], 6 * 16)
            v.tensor_copy(wqkv_hi[:, :], wqkv[:, :])
            v.tensor_copy(wqkv_rest[:, :], wqkv_tail[:, :]).then_inc(s["weights"], 1)
            dve.wait_ge(s["weights"], 1)
            v.tensor_tensor(wqkv_lo[:, :], wqkv[:, :], wqkv_hi[:, :].bitcast(F32), ALU.subtract)
            v.tensor_tensor(wqkv_rest[2 * KB:3 * KB, :], wqkv_tail[2 * KB:3 * KB, :],
                            wqkv_rest[2 * KB:3 * KB, :].bitcast(F32), ALU.subtract).then_inc(s["weights"], 1)
            normalize(2, 0, "t_ready", "scaled")
            first_statistics(1)
            first_statistics(2)
            copies(0, 0)
            residuals(0, 0)
            first_statistics(3)
            dve.wait_ge(s["stats"], 4)
            moments(2, st1, XG, NB)
            evacuate_T(0, 0, 0)
            evacuate_T(0, 0, 1)
            inverse_deviation(2, XG, NB)

            def normalize2(j):
                for t in range(2):
                    normalize(2 * j + t, t, "t2_ready", "scaled2")

            def evacuate_y2(j, q):
                for t in range(2):
                    b = 2 * j + t
                    dve.wait_ge(s["xT2_done"], b + 1)
                    if t == 0:
                        if due(FC * j - FC):
                            dve.wait_ge(s["w1_done"], FC * j - FC)
                    v.tensor_copy(yT[q][:, 0:2, t * 128:(t + 1) * 128],
                                  bank[t][:, 0:256].rearrange("p (c t) -> p c t", c=2))
                    v.tensor_copy(yT[q][0:3 * KB, 2, t * 128:(t + 1) * 128], bank[t][0:3 * KB, 256:384])\
                        .then_inc(s["yT2_ready"], 1)

            def step(i, u, behind, more):
                if more >= 1:
                    residuals(*later(i, u, 1))
                if more >= 0:
                    maxima(i, u, 0)
                    maxima_high(i, u, 0)
                if behind >= 2:
                    invert_sums(*later(i, u, -2))
                if more >= 0:
                    maxima_low(i, u, 0)
                if behind >= 2:
                    divide(*later(i, u, -2))
                if more >= 1:
                    copies(*later(i, u, 1))
                if more >= 0:
                    maxima(i, u, 1)
                    maxima_high(i, u, 1)
                    maxima_low(i, u, 1)
                if more < 0:
                    evacuate_y2(0, 0)
                if behind >= 2:
                    gate_attention(*later(i, u, -2))
                if more >= 1:
                    evacuate_T(*later(i, u, 1), 0)
                if behind >= 2:
                    add_attention(*later(i, u, -2))
                if more >= 3:
                    ib, ub = later(i, u, 3)
                    normalize(4 * ib + ub, ub % 2, "t_ready", "scaled")
                if more >= 1:
                    evacuate_T(*later(i, u, 1), 1)
                if behind >= 2:
                    statistics(*later(i, u, -2))
                if more == 2:
                    dve.wait_ge(s["stats2"], NEARLY)
                    moments(3, st2, 0, NEARLY)
                if more == 1:
                    inverse_deviation(3, 0, NEARLY)
                    normalize2(0)
                if more < 0:
                    normalize2(1)

            sequences(dve, step)
            invert_sums(*LAST)
            divide(*LAST)
            gate_attention(*LAST)
            normalize2(2)
            add_attention(*LAST)
            statistics(*LAST)
            dve.wait_ge(s["stats2"], NB)
            moments(4, st2, NEARLY, NB)

            def add_mlp(j):
                for t in range(2):
                    b = 2 * j + t
                    dve.wait_ge(s["w2_done"], b + 1)
                    dve.wait_ge(s[f"bcg_in{t}"], 16 * (NPAIR + 1) + 16 * j)
                    if due(b - 1):
                        dve.wait_ge(s["result_ready"], b - 1)
                    v.tensor_tensor(gated2[t][:, :], bank[5 + t][:, 0:D], bcg[t][:, :], ALU.mult)\
                        .then_inc(s["gated2_ready"], 1)
                for t in range(2):
                    b = 2 * j + t
                    dve.wait_ge(s["gated2_ready"], b + 1)
                    row = xr[:, bass.ds(b, 1), :]
                    v.tensor_tensor(row, row, gated2[t][:, :].unsqueeze(1), ALU.add).then_inc(s["result_ready"], 1)

            def pair(j, q, front, ahead):
                if ahead and not (isinstance(j, int) and j == 0):
                    normalize2(j + 2)
                if front:
                    evacuate_y2(j + 1, 1 - q)
                add_mlp(j)

            pair(0, 0, True, True)
            inverse_deviation(4, NEARLY, NB)
            with dve.Fori(0, (NPAIR - 4) // 2) as k:
                pair(2 * k + 1, 1, True, True)
                pair(2 * k + 2, 0, True, True)
            pair(NPAIR - 3, 1, True, True)
            pair(NPAIR - 2, 0, True, False)
            pair(NPAIR - 1, 1, False, False)

        @block.tensor
        def _(pe):
            mmul = nc.tensor.matmul
            tr = nc.tensor.transpose
            pe.wait_ge(s["vconsts"], 1)
            pe.wait_ge(s["identities"], 2)
            pe.wait_ge(s["cond_act"], 1)
            tr(bank[0][:, 0:NB], cond_silu[:, 0:KA], identf[0:NB, 0:NB])
            tr(bank[0][0:KB + 1, NB:2 * NB], cond_silu[:, KA:D + 1], identf[0:NB, 0:NB]).then_inc(s["cond_T"], 1)
            pe.wait_ge(s["condT_ev"], 1)
            pe.wait_ge(s["wa_in"], 48)
            for n in range(2):
                cols = slice(n * 3 * D, (n + 1) * 3 * D)
                mmul(bank[1 + n][0:NB, 0:3 * D], condT[:, 0, :], wa_a[:, cols], start=True, stop=False)
                mmul(bank[1 + n][0:NB, 0:3 * D], condT[0:KB + 1, 1, :], wa_b[:, cols],
                     start=False, stop=True).then_inc(s["mod_mm"], 1)

            def transpose_y(dst, src):
                tr(dst[:, 0:128], src[:, 0:KA].bitcast(F32), identf[:, :])
                tr(dst[:, 128:256], src[:, Y_LO_A:YW].bitcast(F32), identf[:, :])
                return tr(dst[0:3 * KB, 256:384], src[:, KA:KA + 3 * KB].bitcast(F32), identf[:, :])

            def front_x(i, u):
                b, p = 4 * i + u, u % 2
                pe.wait_ge(s["y_ready"], b + 1)
                if due(2 * b - 3):
                    pe.wait_ge(s["mT_ev"], 2 * b - 3)
                transpose_y(bank[B_XT], y3[p]).then_inc(s["xT_done"], 1)

            def front_qkv(i, u):
                b, p = 4 * i + u, u % 2
                pe.wait_ge(s["yT_ready"], b + 1)
                if due(2 * b - 2):
                    pe.wait_ge(s["mT_ev"], 2 * b - 2)
                dst = bank[B_QKV][:, 0:3 * D]
                mmul(dst, yT[p][:, 0, 0:128], wqkv_hi[:, :], start=True, stop=False)
                mmul(dst, yT[p][:, 0, 0:128], wqkv_lo[:, :], start=False, stop=False)
                mmul(dst, yT[p][:, 1, 0:128], wqkv_hi[:, :], start=False, stop=False)
                mmul(dst, yT[p][0:3 * KB, 2, 0:128], wqkv_rest[:, :], start=False, stop=True)\
                    .then_inc(s["qkv_done"], 1)

            def front_T(i, u, w):
                b, p = 4 * i + u, u % 2
                if w == 0:
                    pe.wait_ge(s["stack_ready"], b + 1)
                    pe.wait_ge(s["dup_ready"], b + 1)
                    if due(b):
                        pe.wait_ge(s["kTev"], b)
                else:
                    pe.wait_ge(s["qTev"], b + 1)
                dst = bank[B_QKT][:, :].bitcast(BF16)
                for j in range(HH):
                    src = stack[p][:, (w * H + 2 * j) * HS:(w * H + 2 * j + 2) * HS]
                    last = tr(dst[:, j * 128:(j + 1) * 128], src, identb[:, :])
                last.then_inc(s[("qT_done", "kT_done")[w]], 1)

            def operand(u, w, head, rows):
                r = 64 * (head % 2)
                return qkT[u][r:r + rows, w, head // 2, :]

            def scores_by_query(i, u, h):
                b = 4 * i + u
                if h == 0:
                    pe.wait_ge(s["kTev"], b + 1)
                for n, k in enumerate(S_BANK):
                    last_max = 4 * b + 2 * h + n - 1
                    if due(last_max):
                        pe.wait_ge(s["max_done"], last_max)
                    mmul(bank[k][:, :].rearrange("p (h t) -> p h t", t=128), identb[:, :],
                         mask[:, :].unsqueeze(1).to_broadcast([128, HH // 2, 128]),
                         start=True, stop=False, skip_group_check=True)
                    for c in range(HH // 2):
                        head = h * HH + 2 * c + n
                        last = mmul(bank[k][:, c * 128:(c + 1) * 128], operand(u, 0, head, M_ROW), operand(u, 1, head, M_ROW),
                                    start=False, stop=True, skip_group_check=True)
                    last.then_inc(s["s_done"], 1)

            def transpose_m(i, u, h, front):
                b = 4 * i + u
                pe.wait_ge(s["mm_ready"], 2 * b + h + 1)
                if h == 0:
                    pe.wait_ge(s["yT_ready"], b + 2 if front else NB)
                elif front:
                    pe.wait_ge(s["resid_ready"], b + 2)
                    pe.wait_ge(s["v_ready"], b + 2)
                tr(m_slot[h], mm[h][:, :, :, :].rearrange("p n w c -> p (n w c)"), identb[:, :]).then_inc(s["mT_done"], 1)

            def scores_by_key(i, u, h, n):
                b = 4 * i + u
                k = ST_BANK[n]
                if n == 0:
                    pe.wait_ge(s[f"m_placed{h}"], 32 * b + 32)
                last_exp = 4 * b + 2 * h + n - 1
                if due(last_exp):
                    pe.wait_ge(s["exp_done"], last_exp)
                for c in range(HH // 2):
                    head = h * HH + 2 * c + n
                    last = mmul(bank[k][:, c * 128:(c + 1) * 128], operand(u, 1, head, M_ROW + 2),
                                operand(u, 0, head, M_ROW + 2), start=True, stop=True)
                last.then_inc(s["st_done"], 1)

            def weigh(i, u, h):
                b = 4 * i + u
                pe.wait_ge(s["p_ready"], 2 * b + h + 1)
                if h == 0:
                    if due(b):
                        pe.wait_ge(s["gated_read"], b)
                for g in range(2):
                    for q in range(4):
                        head = h * HH + 4 * g + q
                        slot = (head % 2) * (HH // 2) + (head % HH) // 2
                        last = mmul(bank[B_CTX][32 * q:32 * q + HD + 1, (2 * h + g) * 128:(2 * h + g + 1) * 128],
                                    vx[u][:, head, :], P[h][:, slot, :], start=True, stop=True)
                last.then_inc(s["pv_done"], 1)

            def context_by_token(i, u):
                b = 4 * i + u
                pe.wait_ge(s["ctxT_ev"], b + 1)
                for g in range(4):
                    last = tr(bank[B_CTX][:, g * 128:(g + 1) * 128], ctxT[:, g, :], identf[:, :])
                last.then_inc(s["tok_done"], 1)

            def context_back(i, u):
                b = 4 * i + u
                pe.wait_ge(s["ctxn_ready"], b + 1)
                tr(bank[B_CTX][:, 0:128], ctxn[:, 0:KA], identf[:, :])
                tr(bank[B_CTX][0:KB + 1, 128:256], ctxn[:, KA:D + 1], identf[:, :]).then_inc(s["back_done"], 1)

            def project(i, u):
                b = 4 * i + u
                pe.wait_ge(s["back_ev"], b + 1)
                mmul(bank[B_CTX][:, 0:D], backT[:, 0, :], wp_a[:, :], start=True, stop=False)
                mmul(bank[B_CTX][:, 0:D], backT[0:KB + 1, 1, :], wp_b[:, :], start=False, stop=True)\
                    .then_inc(s["wp_done"], 1)

            front_x(0, 0)
            pe.wait_ge(s["weights"], 2)
            pe.wait_ge(s["mod_ev"], 4)
            front_qkv(0, 0)
            front_x(0, 1)
            front_T(0, 0, 0)
            front_T(0, 0, 1)
            pe.wait_ge(s["resid_ready"], 1)
            pe.wait_ge(s["v_ready"], 1)
            front_qkv(0, 1)
            pe.wait_ge(s["consts"], 2)
            pe.wait_ge(s["wp_in"], 48)

            def step(i, u, behind, more):
                one, two = later(i, u, -1), later(i, u, -2)
                if more < 0:
                    context_by_token(*two)
                    scores_by_key(*one, 0, 0)
                    scores_by_key(*one, 0, 1)
                    front_x2(0)
                    context_back(*two)
                    scores_by_key(*one, 1, 0)
                    scores_by_key(*one, 1, 1)
                    expand(0, 0, (0,))
                    project(*two)
                    weigh(*one, 0)
                    expand(0, 0, (1, 2))
                    weigh(*one, 1)
                    return
                scores_by_query(i, u, 0)
                if behind >= 1:
                    scores_by_key(*one, 0, 0)
                if behind >= 2:
                    context_by_token(*two)
                if behind >= 1:
                    scores_by_key(*one, 0, 1)
                scores_by_query(i, u, 1)
                if behind >= 1:
                    scores_by_key(*one, 1, 0)
                if behind >= 2:
                    context_back(*two)
                if behind >= 1:
                    scores_by_key(*one, 1, 1)
                transpose_m(i, u, 0, more >= 1)
                if more >= 1:
                    front_T(*later(i, u, 1), 0)
                if behind >= 2:
                    project(*two)
                if more >= 2:
                    front_x(*later(i, u, 2))
                transpose_m(i, u, 1, more >= 1)
                if behind >= 1:
                    weigh(*one, 0)
                if more >= 1:
                    front_T(*later(i, u, 1), 1)
                if more >= 2:
                    front_qkv(*later(i, u, 2))
                if behind >= 1:
                    weigh(*one, 1)

            def front_x2(j):
                if isinstance(j, int) and j == 0:
                    pe.wait_ge(s["mT_ev"], 2 * NB)
                    pe.wait_ge(s["w1_split"], 1)
                    pe.wait_ge(s["w2_in"], 48)
                for t in range(2):
                    b = 2 * j + t
                    pe.wait_ge(s["y2_ready"], b + 1)
                    if due(b - 1):
                        pe.wait_ge(s["yT2_ready"], b - 1)
                    transpose_y(bank[t], y3[t]).then_inc(s["xT2_done"], 1)

            def expand(j, q, chunks):
                pe.wait_ge(s["yT2_ready"], 2 * j + 2)
                for c in chunks:
                    n = 128 if c < FC - 1 else FL
                    f = slice(c * 128, c * 128 + n)
                    dst = bank[H_BANK[c]][0:n, 0:256]
                    before = FC * j + c - 2 if c >= 3 else FC * (j - 1) + (FC - 1, FC, 3)[c]
                    if due(before):
                        pe.wait_ge(s["silu_done"], before)
                    mmul(dst, w1_hi[:, f], yT[q][:, 0, :], start=True, stop=False)
                    mmul(dst, w1_hi[:, f], yT[q][:, 1, :], start=False, stop=False)
                    mmul(dst, w1_lo[:, f], yT[q][:, 0, :], start=False, stop=False)
                    mmul(dst, w1_rest[:, f], yT[q][0:3 * KB, 2, :], start=False, stop=True)\
                        .then_inc(s["w1_done"], 1)

            def contract(j, q):
                for t in range(2):
                    b = 2 * j + t
                    if due(b - 1):
                        pe.wait_ge(s["gated2_ready"], b - 1)
                    for c in range(FC):
                        n = 128 if c < FC - 1 else FL + 1
                        if t == 0:
                            pe.wait_ge(s["silu_done"], FC * j + c + 1)
                        last = mmul(bank[5 + t][:, 0:D], hT[q][0:n, c, t * 128:(t + 1) * 128], w2[0:n, c, :],
                                    start=(c == 0), stop=(c == FC - 1))
                    last.then_inc(s["w2_done"], 1)

            def pair(j, q, front):
                expand(j, q, range(FC))
                if front:
                    front_x2(j + 1)
                contract(j, q)

            sequences(pe, step)
            context_by_token(*LAST)
            context_back(*LAST)
            expand(0, 0, (3,))
            project(*LAST)
            expand(0, 0, (4,))
            front_x2(1)
            contract(0, 0)
            with pe.Fori(0, (NPAIR - 2) // 2) as k:
                pair(2 * k + 1, 1, True)
                pair(2 * k + 2, 0, True)
            pair(NPAIR - 1, 1, False)


_INS = ['x', 'cond_1152', 'L0_cond_Wq', 'L0_cond_Wk', 'L0_cond_Wv', 'L0_cond_Wp', 'L0_cond_bp', 'L0_cond_W1',
        'L0_cond_b1', 'L0_cond_W2', 'L0_cond_b2', 'L0_cond_Wa', 'L0_cond_ba']


def kernel(**inputs):
    import numpy as _np
    import concourse.bacc as _bacc
    from concourse import mybir as _mybir
    from concourse.bass_utils import run_bass_kernel_spmd as _run

    nc = _bacc.Bacc("TRN2", target_bir_lowering=False, num_devices=1)
    arrays, args = {}, []
    for name in _INS:
        a = _np.ascontiguousarray(inputs[name])
        arrays[f"in_{name}"] = a
        args.append(nc.dram_tensor(f"in_{name}", a.shape, _mybir.dt.from_np(a.dtype), kind="ExternalInput").ap())
    out = nc.dram_tensor("out", (NB, T, D), F32, kind="ExternalOutput").ap()
    build(nc, *args, out)
    r = _run(nc, [arrays], core_ids=[0])
    return r.results[0]["out"]
```
